# Optimizing a Trainium2 kernel written in Bass

```python
import numpy as np
import jax
import jax.numpy as jnp

def _softmax(x, axis=-1):
    return jax.nn.softmax(x, axis=axis)

def _gelu(x):
    return jax.nn.gelu(x, approximate=True)

def _silu(x):
    return jax.nn.silu(x)

def _sigmoid(x):
    return jax.nn.sigmoid(x)

def _layernorm(x, axis=-1, eps=1e-05):
    m = jnp.mean(x, axis=axis, keepdims=True)
    v = jnp.var(x, axis=axis, keepdims=True)
    return (x - m) / jnp.sqrt(v + eps)

def _scatter_add(tgt, idx, src, axis=0):
    return tgt.at[idx].add(src)

def _segment_sum(src, seg, n):
    return jax.ops.segment_sum(src, seg, n)
kernel_name = 'mk_decoder_postln_d1_seqx_r4_5496be'

def setup_inputs(seed: int=0):
    np.random.seed(seed)
    _w = jnp.asarray

    def _rec_inputs():
        import jax
        import jax.numpy as jnp
        _rk = jax.random.key(seed)
        x = -0.0003929 + 0.9999 * jax.random.normal(jax.random.fold_in(_rk, 1), (8, 112, 512), jnp.float32)
        _lenS = 112 - jax.random.randint(jax.random.fold_in(_rk, 7), (8,), 0, max(1, 112 // 4) + 1, jnp.int32)
        _lenS2 = 375 - jax.random.randint(jax.random.fold_in(_rk, 8), (8,), 0, max(1, 375 // 4) + 1, jnp.int32)
        _ctx_1024P = jax.random.normal(jax.random.fold_in(_rk, 11), (8, 16, 256), jnp.float32)
        _ctx_1024c = jax.random.dirichlet(jax.random.fold_in(_rk, 511), 0.3 * jnp.ones((16,), jnp.float32), (8, 375))
        _ctx_1024t = jnp.einsum('bsk,bkd->bsd', _ctx_1024c, _ctx_1024P)
        _ctx_1024t = _ctx_1024t * jax.lax.rsqrt(jnp.mean(jnp.square(_ctx_1024t)) + 1e-12) * 0.953939
        ctx_1024 = 0.000227908 + 0.99994 * (_ctx_1024t + 0.3 * jax.random.normal(jax.random.fold_in(_rk, 611), (8, 375, 256), jnp.float32))
        return (x, ctx_1024)
    x, ctx_1024 = _rec_inputs()

    def _L0_attn_setup():
        import jax, jax.numpy as jnp
        import numpy as np
        DIM = 512
        N_HEADS = 16
        HEAD_DIM = DIM // N_HEADS
        WINDOW = 64
        B, S = (2, 512)
        key = jax.random.key(seed)
        kx, kq, kk, kv, ko = jax.random.split(key, 5)
        bound = 1.0 / np.sqrt(DIM)
        x = jax.random.normal(kx, (B, S, DIM), dtype=jnp.float32)
        wq = jax.random.uniform(kq, (DIM, DIM), jnp.float32, -bound, bound)
        wk = jax.random.uniform(kk, (DIM, DIM), jnp.float32, -bound, bound)
        wv = jax.random.uniform(kv, (DIM, DIM), jnp.float32, -bound, bound)
        wo = jax.random.uniform(ko, (DIM, DIM), jnp.float32, -bound, bound)
        return {'x': x, 'wq': wq, 'wk': wk, 'wv': wv, 'wo': wo}
    _L0_attn_all = _L0_attn_setup()
    _L0_attn_in = {k: v for k, v in _L0_attn_all.items() if k in ('wq', 'wk', 'wv', 'wo')}
    del _L0_attn_all

    def _L0_xattn_setup():
        import jax, jax.numpy as jnp
        import numpy as np
        EPS = 1e-05

        def rmsnorm(x, g, eps=EPS):
            var = jnp.mean(jnp.square(x), axis=-1, keepdims=True)
            return x * jax.lax.rsqrt(var + eps) * g
        key = jax.random.key(seed)
        ks = jax.random.split(key, 8)
        B, Sq, Skv = (2, 1024, 128)
        dim, cdim, H, D = (512, 256, 16, 128)
        inner = H * D
        s = lambda f: 1.0 / np.sqrt(f)
        return {'hidden_states': jax.random.normal(ks[0], (B, Sq, dim), jnp.float32), 'encoder_hidden_states': jax.random.normal(ks[1], (B, Skv, cdim), jnp.float32), 'Wq': jax.random.normal(ks[2], (dim, inner), jnp.float32) * s(dim), 'Wk': jax.random.normal(ks[3], (cdim, inner), jnp.float32) * s(cdim), 'Wv': jax.random.normal(ks[4], (cdim, inner), jnp.float32) * s(cdim), 'Wo': jax.random.normal(ks[5], (inner, dim), jnp.float32) * s(inner), 'gq': jnp.ones((D,), jnp.float32), 'gk': jnp.ones((D,), jnp.float32)}
    _L0_xattn_all = _L0_xattn_setup()
    _L0_xattn_in = {k: v for k, v in _L0_xattn_all.items() if k in ('Wq', 'Wk', 'Wv', 'Wo', 'gq', 'gk')}
    del _L0_xattn_all

    def _L0_ffn_setup():
        import jax, jax.numpy as jnp
        import numpy as np
        TOPK = 2
        N_EXPERTS = 8
        ROUTE_SCALE = 1.0
        key = jax.random.key(seed)
        ks = jax.random.split(key, 7)
        B, T, C = (4, 512, 512)
        H = 352
        HS = 704
        E = N_EXPERTS
        s = 0.02
        return {'x': jax.random.normal(ks[0], (B, T, C), jnp.float32), 'gate_w': jax.random.normal(ks[1], (E, C), jnp.float32) * s, 'gate_bias': jnp.zeros((E,), jnp.float32), 'shared_gw': jax.random.normal(ks[2], (2 * HS, C), jnp.float32) * s, 'shared_dw': jax.random.normal(ks[3], (C, HS), jnp.float32) * s, 'up_w': jax.random.normal(ks[4], (E, 2 * H, C), jnp.float32) * s, 'down_w': jax.random.normal(ks[5], (E, C, H), jnp.float32) * s}
    _L0_ffn_all = _L0_ffn_setup()
    _L0_ffn_in = {k: v for k, v in _L0_ffn_all.items() if k in ('gate_w', 'gate_bias', 'shared_gw', 'shared_dw', 'up_w', 'down_w')}
    del _L0_ffn_all
    return {'x': x, 'ctx_1024': ctx_1024, 'L0_attn_wq': _L0_attn_in['wq'], 'L0_attn_wk': _L0_attn_in['wk'], 'L0_attn_wv': _L0_attn_in['wv'], 'L0_attn_wo': _L0_attn_in['wo'], 'L0_xattn_Wq': _L0_xattn_in['Wq'], 'L0_xattn_Wk': _L0_xattn_in['Wk'], 'L0_xattn_Wv': _L0_xattn_in['Wv'], 'L0_xattn_Wo': _L0_xattn_in['Wo'], 'L0_xattn_gq': _L0_xattn_in['gq'], 'L0_xattn_gk': _L0_xattn_in['gk'], 'L0_ffn_gate_w': _L0_ffn_in['gate_w'], 'L0_ffn_gate_bias': _L0_ffn_in['gate_bias'], 'L0_ffn_shared_gw': _L0_ffn_in['shared_gw'], 'L0_ffn_shared_dw': _L0_ffn_in['shared_dw'], 'L0_ffn_up_w': _L0_ffn_in['up_w'], 'L0_ffn_down_w': _L0_ffn_in['down_w']}

def reference(x, ctx_1024, L0_attn_wq, L0_attn_wk, L0_attn_wv, L0_attn_wo, L0_xattn_Wq, L0_xattn_Wk, L0_xattn_Wv, L0_xattn_Wo, L0_xattn_gq, L0_xattn_gk, L0_ffn_gate_w, L0_ffn_gate_bias, L0_ffn_shared_gw, L0_ffn_shared_dw, L0_ffn_up_w, L0_ffn_down_w):
    import jax
    import jax.numpy as jnp

    def _L0_attn_ref(x, wq, wk, wv, wo):
        import jax, jax.numpy as jnp
        import numpy as np
        DIM = 512
        N_HEADS = 16
        HEAD_DIM = DIM // N_HEADS
        WINDOW = 64
        B, S = (2, 512)
        b, s, d = x.shape
        scale = HEAD_DIM ** (-0.5)
        q = (x @ wq.T).reshape(b, s, N_HEADS, HEAD_DIM)
        k = (x @ wk.T).reshape(b, s, N_HEADS, HEAD_DIM)
        v = (x @ wv.T).reshape(b, s, N_HEADS, HEAD_DIM)
        scores = jnp.einsum('bihd,bjhd->bhij', q, k) * scale
        idx = jnp.arange(s)
        mask = idx[None, :] - idx[:, None] > WINDOW // 2
        scores = jnp.where(mask[None, None, :, :], -jnp.inf, scores)
        attn = jax.nn.softmax(scores, axis=-1)
        out = jnp.einsum('bhij,bjhd->bihd', attn, v).reshape(b, s, d)
        return out @ wo.T

    def _L0_xattn_ref(hidden_states, encoder_hidden_states, Wq, Wk, Wv, Wo, gq, gk):
        import jax, jax.numpy as jnp
        import numpy as np
        EPS = 1e-05

        def rmsnorm(x, g, eps=EPS):
            var = jnp.mean(jnp.square(x), axis=-1, keepdims=True)
            return x * jax.lax.rsqrt(var + eps) * g
        B, Sq, _ = hidden_states.shape
        Skv = encoder_hidden_states.shape[1]
        D = gq.shape[0]
        H = Wq.shape[1] // D
        scale = 1.0 / np.sqrt(D)
        q = (hidden_states @ Wq).reshape(B, Sq, H, D)
        k = (encoder_hidden_states @ Wk).reshape(B, Skv, H, D)
        v = (encoder_hidden_states @ Wv).reshape(B, Skv, H, D)
        q = rmsnorm(q, gq)
        k = rmsnorm(k, gk)
        scores = jnp.einsum('bqhd,bkhd->bhqk', q, k) * scale
        attn = jax.nn.softmax(scores, axis=-1)
        out = jnp.einsum('bhqk,bkhd->bqhd', attn, v)
        out = out.reshape(B, Sq, H * D)
        return out @ Wo

    def _L0_ffn_ref(x, gate_w, gate_bias, shared_gw, shared_dw, up_w, down_w):
        import jax, jax.numpy as jnp
        import numpy as np
        TOPK = 2
        N_EXPERTS = 8
        ROUTE_SCALE = 1.0
        B, T, C = x.shape
        xf = x.reshape(-1, C)
        yg = xf @ shared_gw.T
        y, g = jnp.split(yg, 2, axis=-1)
        shared = jax.nn.silu(g) * y @ shared_dw.T
        scores = jax.nn.sigmoid(xf @ gate_w.T)
        _, topk_idx = jax.lax.top_k(scores + gate_bias, TOPK)
        w = jnp.take_along_axis(scores, topk_idx, axis=-1)
        w = w / jnp.sum(w, axis=-1, keepdims=True) * ROUTE_SCALE
        out = jnp.zeros_like(xf)
        for e in range(N_EXPERTS):
            we = jnp.sum(jnp.where(topk_idx == e, w, 0.0), axis=-1)
            gu = xf @ up_w[e].T
            g_e, u_e = jnp.split(gu, 2, axis=-1)
            h = jax.nn.silu(g_e) * u_e
            out = out + h @ down_w[e].T * we[:, None]
        return (shared + out).reshape(B, T, C)
    x = _layernorm(x + _L0_attn_ref(x, L0_attn_wq, L0_attn_wk, L0_attn_wv, L0_attn_wo), axis=-1)
    x = _layernorm(x + _L0_xattn_ref(x, ctx_1024, L0_xattn_Wq, L0_xattn_Wk, L0_xattn_Wv, L0_xattn_Wo, L0_xattn_gq, L0_xattn_gk), axis=-1)
    x = _layernorm(x + _L0_ffn_ref(x, L0_ffn_gate_w, L0_ffn_gate_bias, L0_ffn_shared_gw, L0_ffn_shared_dw, L0_ffn_up_w, L0_ffn_down_w), axis=-1)
    return x

_drawn_inputs = setup_inputs


def setup_inputs(seed=0):
    import zlib

    import numpy as np

    out = dict(_drawn_inputs(seed))
    spreads = {'L0_xattn_gq': (1.0, 0.2), 'L0_xattn_gk': (1.0, 0.2), 'L0_ffn_gate_bias': (0.0, 0.318)}
    factors = {'L0_attn_wq': 3.611, 'L0_attn_wk': 3.188}
    for name, (base, spread) in spreads.items():
        noise = np.random.default_rng([zlib.crc32(name.encode()), seed]).standard_normal(out[name].shape)
        drawn = base * np.exp(spread * noise) if base else spread * noise
        out[name] = jnp.asarray(drawn.astype(out[name].dtype))
    for name, factor in factors.items():
        out[name] = (out[name] * factor).astype(out[name].dtype)
    return out
```

```python
from contextlib import ExitStack

import concourse.bass as bass
from concourse import mybir

F32 = mybir.dt.float32
F32R = mybir.dt.float32r
U32 = mybir.dt.uint32
ALU = mybir.AluOpType
ACT = mybir.ActivationFunctionType
AX_X = mybir.AxisListType.X

P = 128
BANK = 512
B, T, D = 8, 112, 512
TOK = B * T
DC = D // P
HALF = B // 2
HT = HALF * T
LN_EPS = 1e-5
RMS_EPS = 1e-5
MASKED = -1.0e30

SA_HEADS, SA_DH, WINDOW = 16, 32, 64
QUAD = P // SA_DH
QUADS = SA_HEADS // QUAD
SA_SCALE = float(SA_DH) ** -0.5

XA_HEADS, XA_DH = 16, 128
KV, CD = 375, 256
CC = CD // P
KT_N = 3
KT = KV // KT_N
KVP = KV + 1
PAIRS = XA_HEADS // 2
PW = 2 * XA_DH
XA_SCALE = float(XA_DH) ** -0.5

EXPERTS, HID, SHARED = 8, 352, 704
UNITS_E = EXPERTS + SHARED // HID
HID_TILES = [(0, P), (P, P), (2 * P, HID - 2 * P)]
HC = len(HID_TILES)
UPS = 2 * HC


def hold(eng, sem, i, per, n):
    if isinstance(i, int) and i * per + n <= 0:
        return
    eng.wait_ge(sem, i * per + n)


def run_slots(eng, slot, head, lag, groups):
    for s in range(head):
        slot(s, 0)
    with eng.Fori(0, groups - 1) as i:
        for s in range(head, head + B):
            slot(s, i)
    for s in range(head + B * (groups - 1), lag + B * groups):
        slot(s, 0)


def round_high(pool, hi, raw, zero):
    zeros = zero[0:raw.shape[0], 0:1]
    if len(raw.shape) == 3:
        zeros = zeros.unsqueeze(2)
    return pool.tensor_tensor(hi, raw, zeros.broadcast_to(list(raw.shape)), ALU.add)


def three_products(pe, out, st_hi, st_lo, mv_hi, mv_lo, first, last):
    pe.matmul(out, st_hi, mv_hi, start=first, stop=False)
    pe.matmul(out, st_lo, mv_hi, start=False, stop=False)
    return pe.matmul(out, st_hi, mv_lo, start=False, stop=last)


def layer_norm_stages(nc, env, sem):
    resid, st, mv, rstd, half = env["resid"], env["ln_stats"], env["ln_mv"], env["ln_rstd"], env["neg_half"]

    def stats(dve):
        for b in range(B):
            dve.bn_stats(st[0:T, b, :], resid[0:T, b, :]).then_inc(sem["ln_stat"], 1)
            dve.wait_ge(sem["ln_stat"], b + 1)
            dve.bn_aggr(mv[0:T, b, :], st[0:T, b, :]).then_inc(sem["ln_mean"], 1)

    def power(pool):
        pool.wait_ge(sem["ln_mean"], B)
        pool.tensor_scalar(rstd[0:T, :], mv[0:T, :, 1], LN_EPS, None, ALU.add).then_inc(sem["ln_pow"], 1)
        pool.wait_ge(sem["ln_pow"], 1)
        pool.tensor_tensor(rstd[0:T, :], rstd[0:T, :], half[0:T, 0:B], ALU.pow).then_inc(sem["ln_pow"], 1)

    def apply(dve):
        dve.wait_ge(sem["ln_pow"], 2)
        for b in range(B):
            dve.tensor_scalar(resid[0:T, b, :], resid[0:T, b, :], mv[0:T, b, 0:1], rstd[0:T, b:b + 1],
                              ALU.subtract, ALU.mult).then_inc(sem["ln_done"], 1)

    return stats, power, apply


def turn_stages(nc, env, sem, bank):
    resid, hi, lo, ident = env["resid"], env["xT_hi"], env["xT_lo"], env["ident"]
    view = bank[:, 0:DC * T].rearrange("p (c t) -> p c t", c=DC)

    def turn(pe, b):
        pe.wait_ge(sem["ln_done"], b + 1)
        if b:
            pe.wait_ge(sem["turn_lo"], b)
        for c in range(DC):
            mm = pe.transpose(bank[:, c * T:(c + 1) * T], resid[0:T, b, c * P:(c + 1) * P], ident[0:T, 0:T])
        mm.then_inc(sem["turned"], 1)

    def high(act, b):
        act.wait_ge(sem["turned"], b + 1)
        act.copy(hi[:, :, b * T:(b + 1) * T], view).then_inc(sem["turn_hi"], 1)

    def low(dve, b):
        dve.wait_ge(sem["turn_hi"], b + 1)
        dve.tensor_tensor(lo[:, :, b * T:(b + 1) * T], view, hi[:, :, b * T:(b + 1) * T].bitcast(F32),
                          ALU.subtract).then_inc(sem["turn_lo"], 1)

    return turn, high, low


LN_SEMS = ["ln_stat", "ln_mean", "ln_pow", "ln_done"]
TURN_SEMS = ["turned", "turn_hi", "turn_lo"]


def self_attention(nc, env, xT, x, ctxT, wvT, w_quads):
    LAG, HEAD = 4, 5
    N = QUADS * B
    resid, xT_hi, xT_lo, ident = env["resid"], env["xT_hi"], env["xT_lo"], env["ident"]
    ctx_hi, ctx_lo = env["ctx_hi"], env["ctx_lo"]
    with ExitStack() as es:
        def sb(name, shape, dt=F32):
            return es.enter_context(nc.sbuf_tensor("sa_" + name, shape, dt))

        def ps(name, shape):
            return es.enter_context(nc.psum_tensor("sa_" + name, shape, F32))

        xT_raw = sb("xT_raw", [P, DC, TOK])
        ctx_raw = sb("ctx_raw", [P, CC, B // 2 * KV])
        wv_raw = sb("wv_raw", [P, DC, D])
        wv_hi, wv_lo = sb("wv_hi", [P, DC, D], F32R), sb("wv_lo", [P, DC, D], F32R)
        w_raw = sb("w_raw", [P, 3, D])
        w_hi, w_lo = sb("w_hi", [P, 3, D], F32R), sb("w_lo", [P, 3, D], F32R)
        V = sb("V", [P, B, D])
        qT, kT = sb("qT", [P, TOK]), sb("kT", [P, TOK])
        mask = sb("mask", [P, QUAD, T])
        masked = sb("masked", [P, 2, QUAD, T])
        probs = sb("probs", [P, 4, QUAD, T])
        probsT = sb("probsT", [P, 2, QUAD * T])
        o_nat = sb("o_nat", [P, 2, P])
        oT_hi, oT_lo = sb("oT_hi", [P, 2, T], F32R), sb("oT_lo", [P, 2, T], F32R)
        row_max, neg_max = sb("row_max", [P, 4, QUAD]), sb("neg_max", [P, 4, QUAD])
        row_sum, inv_sum = sb("row_sum", [P, 4, QUAD]), sb("inv_sum", [P, 4, QUAD])

        scores_ps = ps("scores_ps", [P, QUAD, BANK])
        probsT_ps = ps("probsT_ps", [P, BANK])
        o_ps = ps("o_ps", [P, BANK])
        y_ps = ps("y_ps", [P, BANK])
        proj_ps = ps("proj_ps", [P, BANK])

        names = """x_loaded xT_loaded wv_loaded qk_loaded wo_loaded ctx_loaded xT_hi_done xT_lo_done wv_hi_done wv_lo_done
            consts_set ctx_hi_done ctx_lo_done v_ready v_copied proj_ready proj_copied qk_hi_done qk_lo_done wo_hi_done
            wo_lo_done scores_ready masked_done max_ready negmax_ready exp_done probsT_ready probsT_copied o_ready inv_ready
            o_scaled oT_ready oT_hi_done oT_lo_done y_ready y_added""".split()
        sem = {n: es.enter_context(nc.semaphore("sa_" + n)) for n in names}
        block = es.enter_context(nc.Block())

        def split_qk_hi(pool, i, q):
            hold(pool, sem["qk_loaded"], i, 16, 16 * (q + 1))
            hold(pool, sem["proj_ready"], i, 4, 4 * q)
            round_high(pool, w_hi[:, 0:2, :], w_raw[:, 0:2, :], env["zero"]).then_inc(sem["qk_hi_done"], 1)

        def split_wo_hi(pool, i, q):
            hold(pool, sem["wo_loaded"], i, 16, 16 * (q + 1))
            hold(pool, sem["y_ready"], i, B, B * q)
            round_high(pool, w_hi[:, 2, :], w_raw[:, 2, :], env["zero"]).then_inc(sem["wo_hi_done"], 1)

        def proj_in(s):
            p = {1: 2, 2: 3, 6: 4, 7: 5}.get(s % B)
            if p is None or 4 * (s // B) + p >= 4 * QUADS:
                return None
            return 4 * (s // B) + p

        @block.sync
        def _(sp):
            sp.dma_start(wv_raw[:], wvT).then_inc(sem["wv_loaded"], 16)
            sp.dma_start(xT_raw[:], xT).then_inc(sem["xT_loaded"], 16)
            sp.dma_start(w_raw[:, 0:2, :], w_quads[0, :, 0:2, :]).then_inc(sem["qk_loaded"], 16)
            sp.dma_start(w_raw[:, 2, :], w_quads[0, :, 2, :]).then_inc(sem["wo_loaded"], 16)
            sp.dma_start(resid[0:T, :, :], x).then_inc(sem["x_loaded"], 16)
            sp.dma_start(ctx_raw[:], ctxT[:, :, 0:B // 2 * KV]).then_inc(sem["ctx_loaded"], 16)
            sp.wait_ge(sem["ctx_lo_done"], 1)
            sp.dma_start(ctx_raw[:], ctxT[:, :, B // 2 * KV:B * KV]).then_inc(sem["ctx_loaded"], 16)
            with sp.Fori(1, QUADS) as q:
                sp.wait_ge(sem["qk_lo_done"], q)
                sp.dma_start(w_raw[:, 0:2, :], w_quads[q, :, 0:2, :]).then_inc(sem["qk_loaded"], 16)
                sp.wait_ge(sem["wo_lo_done"], q)
                sp.dma_start(w_raw[:, 2, :], w_quads[q, :, 2, :]).then_inc(sem["wo_loaded"], 16)

        @block.gpsimd
        def _(pool):
            pool.memset(ident[:], 0.0).then_inc(sem["consts_set"], 1)
            pool.memset(mask[:], 0.0).then_inc(sem["consts_set"], 1)
            pool.memset(env["neg_half"][:], -0.5).then_inc(sem["consts_set"], 1)
            pool.memset(env["ones"][:], 1.0).then_inc(sem["consts_set"], 1)
            pool.memset(env["zero"][:], 0.0).then_inc(sem["consts_set"], 1)
            pool.wait_ge(sem["consts_set"], 5)
            pool.affine_select(out=ident[:], in_=ident[:], compare_op=ALU.not_equal, fill=1.0, base=0,
                               pattern=[[-1, P]], channel_multiplier=1).then_inc(sem["consts_set"], 1)
            pool.affine_select(out=mask[0:T], in_=mask[0:T], compare_op=ALU.is_ge, fill=MASKED, base=WINDOW // 2,
                               pattern=[[0, QUAD], [-1, T]], channel_multiplier=1).then_inc(sem["consts_set"], 1)
            pool.wait_ge(sem["wv_loaded"], 16)
            pool.tensor_copy(wv_hi[:], wv_raw[:]).then_inc(sem["wv_hi_done"], 1)
            split_qk_hi(pool, 0, 0)
            split_wo_hi(pool, 0, 0)
            for half in range(2):
                cols = slice(half * (B // 2) * KV, (half + 1) * (B // 2) * KV)
                pool.wait_ge(sem["ctx_loaded"], 16 * (half + 1))
                pool.tensor_copy(ctx_hi[:, :, cols], ctx_raw[:]).then_inc(sem["ctx_hi_done"], 1)
                pool.wait_ge(sem["ctx_hi_done"], half + 1)
                pool.tensor_tensor(ctx_lo[:, :, cols], ctx_raw[:], ctx_hi[:, :, cols].bitcast(F32),
                                   ALU.subtract).then_inc(sem["ctx_lo_done"], 1)

            def slot(s, i):
                if s % B == 5 and s // B + 1 < QUADS:
                    split_qk_hi(pool, i, s // B + 1)
                if s % B == 4 and s // B >= 1:
                    split_wo_hi(pool, i, s // B)

            run_slots(pool, slot, HEAD, LAG, QUADS)

        @block.scalar
        def _(act):
            act.wait_ge(sem["xT_loaded"], 16)
            for c in range(DC):
                act.copy(xT_hi[:, c, :], xT_raw[:, c, :]).then_inc(sem["xT_hi_done"], 1)
            for b in range(B):
                act.wait_ge(sem["v_ready"], b + 1)
                act.copy(V[0:T, b, :], scores_ps[0:T, b % QUAD, :]).then_inc(sem["v_copied"], 1)

            def proj_out(i, p):
                hold(act, sem["proj_ready"], i, 4, p + 1)
                dst = (qT, kT)[p % 2]
                g = p // 2 % 2
                act.copy(dst[:, g * HT:(g + 1) * HT], proj_ps[:, 0:HT]).then_inc(sem["proj_copied"], 1)

            proj_out(0, 0)
            proj_out(0, 1)

            def slot(s, i):
                u = s - 4
                if u >= 0:
                    hold(act, sem["oT_ready"], i, B, u + 1)
                    hold(act, sem["y_ready"], i, B, u - 1)
                    act.copy(oT_hi[:, u % 2, :], o_ps[:, 0:T]).then_inc(sem["oT_hi_done"], 1)
                u = s - 2
                if 0 <= u < N:
                    hold(act, sem["probsT_ready"], i, B, u + 1)
                    hold(act, sem["o_ready"], i, B, u - 1)
                    act.copy(probsT[0:T, u % 2, :], probsT_ps[0:T, 0:QUAD * T]).then_inc(sem["probsT_copied"], 1)
                p = proj_in(s)
                if p is not None:
                    proj_out(i, p)
                u = s
                if u < N:
                    hold(act, sem["negmax_ready"], i, B, u + 1)
                    hold(act, sem["probsT_ready"], i, B, u - 3)
                    for r in range(QUAD):
                        act.activation(probs[0:T, u % 4, r, :], masked[0:T, u % 2, r, :], ACT.Exp,
                                       bias=neg_max[0:T, u % 4, r:r + 1], scale=SA_SCALE,
                                       accum_out=row_sum[0:T, u % 4, r:r + 1]).then_inc(sem["exp_done"], 1)

            run_slots(act, slot, HEAD, LAG, QUADS)

        @block.vector
        def _(dve):
            dve.wait_ge(sem["wv_hi_done"], 1)
            dve.tensor_tensor(wv_lo[:], wv_raw[:], wv_hi[:].bitcast(F32), ALU.subtract).then_inc(sem["wv_lo_done"], 1)
            for c in range(DC):
                dve.wait_ge(sem["xT_hi_done"], c + 1)
                dve.tensor_tensor(xT_lo[:, c, :], xT_raw[:, c, :], xT_hi[:, c, :].bitcast(F32),
                                  ALU.subtract).then_inc(sem["xT_lo_done"], 1)

            def split_qk_lo(i, q):
                hold(dve, sem["qk_hi_done"], i, 1, q + 1)
                dve.tensor_tensor(w_lo[:, 0:2, :], w_raw[:, 0:2, :], w_hi[:, 0:2, :].bitcast(F32),
                                  ALU.subtract).then_inc(sem["qk_lo_done"], 1)

            def split_wo_lo(i, q):
                hold(dve, sem["wo_hi_done"], i, 1, q + 1)
                dve.tensor_tensor(w_lo[:, 2, :], w_raw[:, 2, :], w_hi[:, 2, :].bitcast(F32),
                                  ALU.subtract).then_inc(sem["wo_lo_done"], 1)

            split_qk_lo(0, 0)
            split_wo_lo(0, 0)
            dve.wait_ge(sem["consts_set"], 7)
            dve.wait_ge(sem["x_loaded"], 16)

            def slot(s, i):
                u = s - 4
                if u >= 0:
                    hold(dve, sem["oT_hi_done"], i, B, u + 1)
                    dve.tensor_tensor(oT_lo[:, u % 2, :], o_ps[:, 0:T], oT_hi[:, u % 2, :].bitcast(F32),
                                      ALU.subtract).then_inc(sem["oT_lo_done"], 1)
                if s % B == 4 and s // B >= 1:
                    split_wo_lo(i, s // B)
                u = s
                if u < N:
                    hold(dve, sem["scores_ready"], i, B, u + 1)
                    hold(dve, sem["exp_done"], i, QUAD * B, QUAD * (u - 1))
                    dve.tensor_tensor(masked[0:T, u % 2], scores_ps[0:T, :, 0:T], mask[0:T],
                                      ALU.add).then_inc(sem["masked_done"], 1)
                    hold(dve, sem["masked_done"], i, B, u + 1)
                    dve.tensor_reduce(row_max[0:T, u % 4, :], masked[0:T, u % 2], AX_X, ALU.max).then_inc(sem["max_ready"], 1)
                    hold(dve, sem["max_ready"], i, B, u + 1)
                    dve.tensor_scalar(neg_max[0:T, u % 4, :], row_max[0:T, u % 4, :], -SA_SCALE, None,
                                      ALU.mult).then_inc(sem["negmax_ready"], 1)
                if s % B == 5 and s // B + 1 < QUADS:
                    split_qk_lo(i, s // B + 1)
                u = s - 2
                if 0 <= u < N:
                    hold(dve, sem["exp_done"], i, QUAD * B, QUAD * (u + 1))
                    dve.reciprocal(inv_sum[0:T, u % 4, :], row_sum[0:T, u % 4, :]).then_inc(sem["inv_ready"], 1)
                u = s - 3
                if 0 <= u < N:
                    hold(dve, sem["o_ready"], i, B, u + 1)
                    hold(dve, sem["inv_ready"], i, B, u + 1)
                    hold(dve, sem["oT_ready"], i, B, u - 1)
                    dve.tensor_tensor(o_nat[0:T, u % 2, :].rearrange("p (h d) -> p h d", h=QUAD),
                                      o_ps[0:T, 0:P].rearrange("p (h d) -> p h d", h=QUAD),
                                      inv_sum[0:T, u % 4, :].unsqueeze(2).broadcast_to([T, QUAD, SA_DH]),
                                      ALU.mult).then_inc(sem["o_scaled"], 1)
                u = s - 4
                if u >= 0:
                    hold(dve, sem["y_ready"], i, B, u + 1)
                    hold(dve, sem["y_added"], i, B, u)
                    dve.tensor_tensor(resid[0:T, u % B, :], resid[0:T, u % B, :], y_ps[0:T, :],
                                      ALU.add).then_inc(sem["y_added"], 1)

            run_slots(dve, slot, HEAD, LAG, QUADS)

        @block.tensor
        def _(pe):
            pe.wait_ge(sem["wv_lo_done"], 1)
            pe.wait_ge(sem["xT_lo_done"], DC)
            for b in range(B):
                if b >= QUAD:
                    pe.wait_ge(sem["v_copied"], b - QUAD + 1)
                cols = slice(b * T, (b + 1) * T)
                for c in range(DC):
                    mm = three_products(pe, scores_ps[0:T, b % QUAD, :], xT_hi[:, c, cols], xT_lo[:, c, cols],
                                        wv_hi[:, c, :], wv_lo[:, c, :], c == 0, c == DC - 1)
                mm.then_inc(sem["v_ready"], 1)

            def project(i, p):
                hold(pe, sem["qk_lo_done"], i, 1, p // 4 + 1)
                hold(pe, sem["proj_copied"], i, 4, p)
                g = p // 2 % 2
                for c in range(DC):
                    w = slice(c * P, (c + 1) * P)
                    mm = three_products(pe, proj_ps[:, 0:HT], w_hi[:, p % 2, w], w_lo[:, p % 2, w],
                                        xT_hi[:, c, g * HT:(g + 1) * HT], xT_lo[:, c, g * HT:(g + 1) * HT],
                                        c == 0, c == DC - 1)
                mm.then_inc(sem["proj_ready"], 1)

            project(0, 0)
            project(0, 1)
            pe.wait_ge(sem["v_copied"], B)
            pe.wait_ge(sem["consts_set"], 7)

            def slot(s, i):
                u = s - 4
                if u >= 0:
                    hold(pe, sem["o_scaled"], i, B, u + 1)
                    pe.transpose(o_ps[:, 0:T], o_nat[0:T, u % 2, :], ident[0:T, 0:T]).then_inc(sem["oT_ready"], 1)
                u = s
                if u < N:
                    hold(pe, sem["proj_copied"], i, 4, 4 * (u // B) + 2 * (u % B // HALF) + 2)
                    hold(pe, sem["masked_done"], i, B, u)
                    cols = slice(u % B * T, (u % B + 1) * T)
                    for r in range(QUAD):
                        rows = slice(r * SA_DH, (r + 1) * SA_DH)
                        mm = pe.matmul(scores_ps[0:T, r, 0:T], qT[rows, cols], kT[rows, cols], start=True, stop=True)
                    mm.then_inc(sem["scores_ready"], 1)
                u = s - 2
                if 0 <= u < N:
                    hold(pe, sem["exp_done"], i, QUAD * B, QUAD * (u + 1))
                    hold(pe, sem["probsT_copied"], i, B, u)
                    for r in range(QUAD):
                        mm = pe.transpose(probsT_ps[0:T, r * T:(r + 1) * T], probs[0:T, u % 4, r, :], ident[0:T, 0:T])
                    mm.then_inc(sem["probsT_ready"], 1)
                p = proj_in(s)
                if p is not None:
                    project(i, p)
                u = s - 3
                if 0 <= u < N:
                    hold(pe, sem["probsT_copied"], i, B, u + 1)
                    hold(pe, sem["oT_lo_done"], i, B, u)
                    for r in range(QUAD):
                        head = (i + u // B) * P + r * SA_DH
                        mm = pe.matmul(o_ps[0:T, r * SA_DH:(r + 1) * SA_DH], probsT[0:T, u % 2, r * T:(r + 1) * T],
                                       V[0:T, u % B, bass.ds(head, SA_DH)], start=True, stop=True)
                    mm.then_inc(sem["o_ready"], 1)
                u = s - 4
                if u >= 0:
                    hold(pe, sem["wo_lo_done"], i, 1, u // B + 1)
                    hold(pe, sem["oT_lo_done"], i, B, u + 1)
                    hold(pe, sem["y_added"], i, B, u)
                    three_products(pe, y_ps[0:T, :], oT_hi[:, u % 2, :], oT_lo[:, u % 2, :], w_hi[:, 2, :], w_lo[:, 2, :],
                                   True, True).then_inc(sem["y_ready"], 1)

            run_slots(pe, slot, HEAD, LAG, QUADS)


def cross_attention(nc, env, w_pairs, gains):
    LAG, HEAD = 3, 3
    N = PAIRS * B
    resid, xT_hi, xT_lo, ident = env["resid"], env["xT_hi"], env["xT_lo"], env["ident"]
    ctx_hi, ctx_lo = env["ctx_hi"], env["ctx_lo"]
    with ExitStack() as es:
        def sb(name, shape, dt=F32):
            return es.enter_context(nc.sbuf_tensor("xa_" + name, shape, dt))

        def ps(name, shape):
            return es.enter_context(nc.psum_tensor("xa_" + name, shape, F32))

        wq_raw, wk_raw, wv_raw, wo_raw = (sb("wq_raw", [P, DC, PW]), sb("wk_raw", [P, CC, PW]),
                                          sb("wv_raw", [P, CC, PW]), sb("wo_raw", [P, 2, D]))
        wq_hi, wq_lo = sb("wq_hi", [P, DC, PW], F32R), sb("wq_lo", [P, DC, PW], F32R)
        wk_hi, wk_lo = sb("wk_hi", [P, CC, PW], F32R), sb("wk_lo", [P, CC, PW], F32R)
        wv_hi, wv_lo = sb("wv_hi", [P, CC, PW], F32R), sb("wv_lo", [P, CC, PW], F32R)
        wo_hi, wo_lo = sb("wo_hi", [P, 2, D], F32R), sb("wo_lo", [P, 2, D], F32R)
        gain_in, gain = sb("gain_in", [P, 2]), sb("gain", [P, 1])
        qT_hi, qT_lo = sb("qT_hi", [P, 2, TOK], F32R), sb("qT_lo", [P, 2, TOK], F32R)
        q_sq = sb("q_sq", [P, 2, HT])
        q_ms, q_scale = sb("q_ms", [P, 2, 2, HALF]), sb("q_scale", [P, 2, 2, HALF])
        k_sq, k_hat = sb("k_sq", [P, KT_N * PW]), sb("k_hat", [P, KT_N * PW])
        k_ss, k_ms, k_inv = sb("k_ss", [P, 2 * KT_N]), sb("k_ms", [P, 2 * KT_N]), sb("k_inv", [P, 2 * KT_N])
        sum_eps = sb("sum_eps", [P, 2 * KT_N])
        kT_hi, kT_lo = sb("kT_hi", [P, 2, KVP], F32R), sb("kT_lo", [P, 2, KVP], F32R)
        V = sb("V", [P, 4, KT_N * PW])
        probs = sb("probs", [P, 2, 2, KV])
        probsT = sb("probsT", [P, 2, 2, KT_N * T])
        oT_hi, oT_lo = sb("oT_hi", [P, 2, 2, T], F32R), sb("oT_lo", [P, 2, 2, T], F32R)
        row_max, bias = sb("row_max", [P, 2, 2]), sb("bias", [P, 2, 2])
        row_sum, inv_sum = sb("row_sum", [P, 2, 2]), sb("inv_sum", [P, 2, 2])

        k01_ps = ps("k01_ps", [P, BANK])
        kv2_ps = ps("kv2_ps", [P, BANK])
        v01_ps = ps("v01_ps", [P, BANK])
        turn_ps = ps("turn_ps", [P, 2, BANK])
        scores_ps = ps("scores_ps", [P, 2, BANK])
        y_ps = ps("y_ps", [P, BANK])

        names = """wq_loaded wk_loaded wv_loaded wo_loaded gains_loaded gain_ready pads_set
            wq_hi_done wq_lo_done wk_hi_done wk_lo_done wv_hi_done wv_lo_done wo_hi_done wo_lo_done
            q_ready q_hi_done q_sq_done q_lo_done qss_ready qms_done q_scale_done
            k_ready k_sq_done kss_done kms_done kinv_done khat_done v_ready v_copied
            kT_ready kT_hi_done kT_lo_done scores_ready max_done bias_ready exp_done inv_done probs_done
            probsT_ready probsT_0_done probsT_1_done o_ready oT_hi_done oT_lo_done y_ready y_added""".split()
        sem = {n: es.enter_context(nc.semaphore("xa_" + n)) for n in names + LN_SEMS + TURN_SEMS}
        ln_stats, ln_power, ln_apply = layer_norm_stages(nc, env, sem)
        turn, turn_high, turn_low = turn_stages(nc, env, sem, y_ps)
        block = es.enter_context(nc.Block())

        def split_hi(pool, i, q, name, raw, hi, done, per, count):
            hold(pool, sem[name + "_loaded"], i, 16, 16 * (q + 1))
            hold(pool, sem[done], i, per, count)
            round_high(pool, hi[:], raw[:], env["zero"]).then_inc(sem[name + "_hi_done"], 1)

        def split_lo(dve, i, q, name, raw, hi, lo):
            hold(dve, sem[name + "_hi_done"], i, 1, q + 1)
            dve.tensor_tensor(lo[:], raw[:], hi[:].bitcast(F32), ALU.subtract).then_inc(sem[name + "_lo_done"], 1)

        def proj_after(s):
            p = {1: 2, 2: 3, 5: 4, 6: 5}.get(s % B)
            if p is None or 4 * (s // B) + p >= 4 * PAIRS:
                return None
            return 4 * (s // B) + p

        def squares_after(s):
            k = {3: 1, 7: 2}.get(s % B)
            if k is None or 2 * (s // B) + k >= 2 * PAIRS:
                return None
            return 2 * (s // B) + k

        @block.sync
        def _(sp):
            loads = ((wk_raw, "wk", slice(4 * PW, 6 * PW)), (wv_raw, "wv", slice(6 * PW, 8 * PW)),
                     (wq_raw, "wq", slice(0, 4 * PW)), (wo_raw, "wo", slice(8 * PW, 12 * PW)))
            for raw, name, cols in loads:
                sp.dma_start(raw[:].rearrange("p a n -> p (a n)"), w_pairs[0, :, cols]).then_inc(sem[name + "_loaded"], 16)
                if name == "wq":
                    sp.dma_start(gain_in[:], gains).then_inc(sem["gains_loaded"], 16)
            with sp.Fori(1, PAIRS) as q:
                for raw, name, cols in loads[2:3] + loads[0:2] + loads[3:4]:
                    sp.wait_ge(sem[name + "_lo_done"], q)
                    sp.dma_start(raw[:].rearrange("p a n -> p (a n)"),
                                 w_pairs[q, :, cols]).then_inc(sem[name + "_loaded"], 16)

        @block.gpsimd
        def _(pool):
            pool.memset(kT_hi[:, :, KV:KVP].bitcast(F32), 0.0).then_inc(sem["pads_set"], 1)
            pool.memset(kT_lo[:, :, KV:KVP].bitcast(F32), 0.0).then_inc(sem["pads_set"], 1)
            pool.memset(sum_eps[:], XA_DH * RMS_EPS).then_inc(sem["pads_set"], 1)
            split_hi(pool, 0, 0, "wk", wk_raw, wk_hi, "k_ready", B, 0)
            split_hi(pool, 0, 0, "wv", wv_raw, wv_hi, "v_ready", 2 * B, 0)
            split_hi(pool, 0, 0, "wq", wq_raw, wq_hi, "q_ready", 4, 0)
            pool.wait_ge(sem["gains_loaded"], 16)
            pool.tensor_scalar(gain[:], gain_in[:, 0:1], gain_in[:, 1:2], XA_SCALE * XA_DH, ALU.mult,
                               ALU.mult).then_inc(sem["gain_ready"], 1)
            ln_power(pool)

            def query_scale(i, k):
                g = k % 2
                hold(pool, sem["qms_done"], i, 2, k + 1)
                hold(pool, sem["exp_done"], i, 2 * B, B * (k - 1))
                pool.tensor_tensor(q_scale[0:T, g], q_ms[0:T, g], env["neg_half"][0:T, 0:2 * HALF].rearrange(
                    "p (a b) -> p a b", a=2), ALU.pow).then_inc(sem["q_scale_done"], 1)

            def slot(s, i):
                if s % B == 0 and 1 <= s // B < PAIRS:
                    split_hi(pool, i, s // B, "wv", wv_raw, wv_hi, "v_ready", 2 * B, 2 * B * (s // B))
                u = s
                if u < N:
                    hold(pool, sem["kss_done"], i, B, u + 1)
                    pool.tensor_tensor(k_ms[0:KT, :], k_ss[0:KT, :], sum_eps[0:KT, :], ALU.add).then_inc(sem["kms_done"], 1)
                    hold(pool, sem["kms_done"], i, B, u + 1)
                    hold(pool, sem["khat_done"], i, 2 * B, 2 * u)
                    pool.tensor_tensor(k_inv[0:KT, :], k_ms[0:KT, :], env["neg_half"][0:KT, 0:2 * KT_N],
                                       ALU.pow).then_inc(sem["kinv_done"], 1)
                if s % B == 3 and s // B + 1 < PAIRS:
                    q = s // B + 1
                    split_hi(pool, i, q, "wq", wq_raw, wq_hi, "q_ready", 4, 4 * q)
                if s % B == 7 and s // B + 1 < PAIRS:
                    q = s // B + 1
                    split_hi(pool, i, q, "wk", wk_raw, wk_hi, "k_ready", 2 * B, 2 * B * q)
                u = s - 1
                if 0 <= u < N:
                    hold(pool, sem["inv_done"], i, B, u + 1)
                    pool.tensor_tensor(probs[0:T, u % 2], probs[0:T, u % 2],
                                       inv_sum[0:T, u % 2, :].unsqueeze(2).broadcast_to([T, 2, KV]),
                                       ALU.mult).then_inc(sem["probs_done"], 1)
                if s % B == 2 and s // B < PAIRS:
                    split_hi(pool, i, s // B, "wo", wo_raw, wo_hi, "y_ready", B, B * (s // B))
                k = squares_after(s)
                if k is not None:
                    query_scale(i, k)
                if s == 0:
                    query_scale(0, 0)

            run_slots(pool, slot, HEAD, LAG, PAIRS)

        @block.scalar
        def _(act):
            def queries_out(i, p):
                g, h = p // 2 % 2, p % 2
                hold(act, sem["q_ready"], i, 4, p + 1)
                act.activation(qT_hi[:, h, g * HT:(g + 1) * HT], y_ps[:, 0:HT], ACT.Copy,
                               scale=gain[:, 0:1]).then_inc(sem["q_hi_done"], 1)
                if h == 0:
                    hold(act, sem["qss_ready"], i, 2, p // 2)
                act.activation(q_sq[:, h, :], y_ps[:, 0:HT], ACT.Square).then_inc(sem["q_sq_done"], 1)

            def slot(s, i):
                u = s
                if u < N:
                    hold(act, sem["k_ready"], i, 2 * B, 2 * u + 1)
                    hold(act, sem["kss_done"], i, B, u)
                    act.activation(k_sq[0:KT, 0:2 * PW], k01_ps[0:KT, :], ACT.Square).then_inc(sem["k_sq_done"], 1)
                    hold(act, sem["k_ready"], i, 2 * B, 2 * u + 2)
                    act.activation(k_sq[0:KT, 2 * PW:3 * PW], kv2_ps[0:KT, 0:PW], ACT.Square).then_inc(sem["k_sq_done"], 1)
                u = s - 1
                if 0 <= u < N:
                    hold(act, sem["kT_ready"], i, B, u + 1)
                    act.copy(kT_hi[:, :, 0:KV], turn_ps[:, :, 0:KV]).then_inc(sem["kT_hi_done"], 1)
                u = s
                if u < N:
                    hold(act, sem["v_ready"], i, 2 * B, 2 * u + 1)
                    hold(act, sem["o_ready"], i, B, u - 3)
                    act.copy(V[0:KT, u % 4, 0:2 * PW], v01_ps[0:KT, :]).then_inc(sem["v_copied"], 1)
                u = s - 2
                if 0 <= u < N:
                    hold(act, sem["probsT_ready"], i, B, u + 1)
                    hold(act, sem["o_ready"], i, B, u - 1)
                    act.copy(probsT[0:KT, u % 2, 0, :], turn_ps[0:KT, 0, 0:KT_N * T]).then_inc(sem["probsT_0_done"], 1)
                u = s - 1
                if 0 <= u < N:
                    hold(act, sem["bias_ready"], i, B, u + 1)
                    hold(act, sem["probsT_ready"], i, B, u - 1)
                    for h in range(2):
                        act.activation(probs[0:T, u % 2, h, :], scores_ps[0:T, h, 0:KV], ACT.Exp,
                                       bias=bias[0:T, u % 2, h:h + 1],
                                       scale=q_scale[0:T, u % B // HALF, h, u % HALF:u % HALF + 1],
                                       accum_out=row_sum[0:T, u % 2, h:h + 1]).then_inc(sem["exp_done"], 1)
                u = s
                if u < N:
                    hold(act, sem["v_ready"], i, 2 * B, 2 * u + 2)
                    act.copy(V[0:KT, u % 4, 2 * PW:3 * PW], kv2_ps[0:KT, PW:2 * PW]).then_inc(sem["v_copied"], 1)
                u = s - 2
                if 0 <= u < N:
                    hold(act, sem["o_ready"], i, B, u + 1)
                    hold(act, sem["y_ready"], i, B, u - 1)
                    act.copy(oT_hi[:, u % 2], turn_ps[:, :, 0:T]).then_inc(sem["oT_hi_done"], 1)
                p = proj_after(s)
                if p is not None:
                    queries_out(i, p)
                if s == 0:
                    for b in range(B):
                        turn_high(act, b)
                    act.wait_ge(sem["gain_ready"], 1)
                    queries_out(0, 0)
                    queries_out(0, 1)

            run_slots(act, slot, HEAD, LAG, PAIRS)

        @block.vector
        def _(dve):
            ln_stats(dve)
            split_lo(dve, 0, 0, "wk", wk_raw, wk_hi, wk_lo)
            split_lo(dve, 0, 0, "wv", wv_raw, wv_hi, wv_lo)
            ln_apply(dve)

            def queries_out(i, p):
                g, h = p // 2 % 2, p % 2
                cols = slice(g * HT, (g + 1) * HT)
                hold(dve, sem["q_sq_done"], i, 4, p + 1)
                dve.scalar_tensor_tensor(out=qT_lo[:, h, cols], in0=y_ps[:, 0:HT], scalar=gain[:, 0:1],
                                         in1=qT_hi[:, h, cols].bitcast(F32), op0=ALU.mult,
                                         op1=ALU.subtract).then_inc(sem["q_lo_done"], 1)

            def mean_squares(i, k):
                hold(dve, sem["qss_ready"], i, 2, k + 1)
                hold(dve, sem["q_scale_done"], i, 2, k - 1)
                dve.tensor_scalar(q_ms[0:T, k % 2].rearrange("p a b -> p (a b)"), y_ps[0:T, 0:2 * HALF], XA_DH * RMS_EPS,
                                  None, ALU.add).then_inc(sem["qms_done"], 1)

            def slot(s, i):
                u = s
                if u < N:
                    hold(dve, sem["k_sq_done"], i, 2 * B, 2 * u + 2)
                    hold(dve, sem["kms_done"], i, B, u)
                    dve.tensor_reduce(k_ss[0:KT, :], k_sq[0:KT, :].rearrange("p (a d) -> p a d", d=XA_DH), AX_X,
                                      ALU.add).then_inc(sem["kss_done"], 1)
                u = s - 1
                if 0 <= u < N:
                    hold(dve, sem["kT_hi_done"], i, B, u + 1)
                    dve.tensor_tensor(kT_lo[:, :, 0:KV], turn_ps[:, :, 0:KV], kT_hi[:, :, 0:KV].bitcast(F32),
                                      ALU.subtract).then_inc(sem["kT_lo_done"], 1)
                if s % B == 0 and 1 <= s // B < PAIRS:
                    split_lo(dve, i, s // B, "wv", wv_raw, wv_hi, wv_lo)
                u = s - 3
                if 0 <= u < N:
                    hold(dve, sem["y_ready"], i, B, u + 1)
                    hold(dve, sem["y_added"], i, B, u)
                    dve.tensor_tensor(resid[0:T, u % B, :], resid[0:T, u % B, :], y_ps[0:T, :],
                                      ALU.add).then_inc(sem["y_added"], 1)
                u = s
                if u < N:
                    hold(dve, sem["kinv_done"], i, B, u + 1)
                    hold(dve, sem["kT_ready"], i, B, u)
                    dve.tensor_tensor(k_hat[0:KT, 0:2 * PW].rearrange("p (a d) -> p a d", d=XA_DH),
                                      k01_ps[0:KT, :].rearrange("p (a d) -> p a d", d=XA_DH),
                                      k_inv[0:KT, 0:4].unsqueeze(2).broadcast_to([KT, 4, XA_DH]),
                                      ALU.mult).then_inc(sem["khat_done"], 1)
                    dve.tensor_tensor(k_hat[0:KT, 2 * PW:3 * PW].rearrange("p (a d) -> p a d", d=XA_DH),
                                      kv2_ps[0:KT, 0:PW].rearrange("p (a d) -> p a d", d=XA_DH),
                                      k_inv[0:KT, 4:6].unsqueeze(2).broadcast_to([KT, 2, XA_DH]),
                                      ALU.mult).then_inc(sem["khat_done"], 1)
                u = s - 1
                if 0 <= u < N:
                    hold(dve, sem["scores_ready"], i, B, u + 1)
                    hold(dve, sem["bias_ready"], i, B, u)
                    dve.tensor_reduce(row_max[0:T, u % 2, :], scores_ps[0:T, :, 0:KV], AX_X, ALU.max).then_inc(sem["max_done"], 1)
                    hold(dve, sem["max_done"], i, B, u + 1)
                    hold(dve, sem["q_scale_done"], i, 2, 2 * (u // B) + u % B // HALF + 1)
                    hold(dve, sem["exp_done"], i, 2 * B, 2 * (u - 1))
                    dve.scalar_tensor_tensor(out=bias[0:T, u % 2, :], in0=row_max[0:T, u % 2, :], scalar=-1.0,
                                             in1=q_scale[0:T, u % B // HALF, :, u % HALF], op0=ALU.mult,
                                             op1=ALU.mult).then_inc(sem["bias_ready"], 1)
                u = s - 2
                if 0 <= u < N:
                    hold(dve, sem["probsT_ready"], i, B, u + 1)
                    hold(dve, sem["o_ready"], i, B, u - 1)
                    dve.tensor_copy(probsT[0:KT, u % 2, 1, :], turn_ps[0:KT, 1, 0:KT_N * T]).then_inc(sem["probsT_1_done"], 1)
                if s % B == 3 and s // B + 1 < PAIRS:
                    split_lo(dve, i, s // B + 1, "wq", wq_raw, wq_hi, wq_lo)
                if s % B == 7 and s // B + 1 < PAIRS:
                    split_lo(dve, i, s // B + 1, "wk", wk_raw, wk_hi, wk_lo)
                u = s - 1
                if 0 <= u < N:
                    hold(dve, sem["exp_done"], i, 2 * B, 2 * (u + 1))
                    hold(dve, sem["probs_done"], i, B, u - 1)
                    dve.reciprocal(inv_sum[0:T, u % 2, :], row_sum[0:T, u % 2, :]).then_inc(sem["inv_done"], 1)
                u = s - 2
                if 0 <= u < N:
                    hold(dve, sem["oT_hi_done"], i, B, u + 1)
                    dve.tensor_tensor(oT_lo[:, u % 2], turn_ps[:, :, 0:T], oT_hi[:, u % 2].bitcast(F32),
                                      ALU.subtract).then_inc(sem["oT_lo_done"], 1)
                if s % B == 2 and s // B < PAIRS:
                    split_lo(dve, i, s // B, "wo", wo_raw, wo_hi, wo_lo)
                p = proj_after(s)
                if p is not None:
                    queries_out(i, p)
                k = squares_after(s)
                if k is not None:
                    mean_squares(i, k)
                if s == 0:
                    for b in range(B):
                        turn_low(dve, b)
                    split_lo(dve, 0, 0, "wq", wq_raw, wq_hi, wq_lo)
                    dve.wait_ge(sem["gain_ready"], 1)
                    queries_out(0, 0)
                    queries_out(0, 1)
                    mean_squares(0, 0)

            run_slots(dve, slot, HEAD, LAG, PAIRS)

        @block.tensor
        def _(pe):
            def project(out, u, tile, w_hi, w_lo):
                cols = slice(u % B * KV + tile * KT, u % B * KV + (tile + 1) * KT)
                for c in range(CC):
                    mm = three_products(pe, out, ctx_hi[:, c, cols], ctx_lo[:, c, cols], w_hi[:, c, :], w_lo[:, c, :],
                                        c == 0, c == CC - 1)
                return mm

            def queries(i, p):
                g, h = p // 2 % 2, p % 2
                hold(pe, sem["wq_lo_done"], i, 1, p // 4 + 1)
                hold(pe, sem["q_lo_done"], i, 4, p)
                for c in range(DC):
                    w = slice(h * XA_DH, (h + 1) * XA_DH)
                    mm = three_products(pe, y_ps[:, 0:HT], wq_hi[:, c, w], wq_lo[:, c, w],
                                        xT_hi[:, c, g * HT:(g + 1) * HT], xT_lo[:, c, g * HT:(g + 1) * HT],
                                        c == 0, c == DC - 1)
                mm.then_inc(sem["q_ready"], 1)

            def sum_squares(i, k):
                hold(pe, sem["q_sq_done"], i, 4, 2 * k + 2)
                hold(pe, sem["q_lo_done"], i, 4, 2 * k + 2)
                for h in range(2):
                    for b in range(HALF):
                        at = h * HALF + b
                        mm = pe.matmul(y_ps[0:T, at:at + 1], q_sq[:, h, b * T:(b + 1) * T], env["ones"][:, 0:1],
                                       start=True, stop=True)
                mm.then_inc(sem["qss_ready"], 1)

            def slot(s, i):
                u = s
                if u < N:
                    hold(pe, sem["wk_lo_done"], i, 1, u // B + 1)
                    hold(pe, sem["khat_done"], i, 2 * B, 2 * u)
                    project(k01_ps[0:KT, 0:PW], u, 0, wk_hi, wk_lo)
                    project(k01_ps[0:KT, PW:2 * PW], u, 1, wk_hi, wk_lo).then_inc(sem["k_ready"], 1)
                    hold(pe, sem["v_copied"], i, 2 * B, 2 * u)
                    project(kv2_ps[0:KT, 0:PW], u, 2, wk_hi, wk_lo).then_inc(sem["k_ready"], 1)
                u = s - 1
                if 0 <= u < N:
                    hold(pe, sem["khat_done"], i, 2 * B, 2 * u + 2)
                    hold(pe, sem["oT_lo_done"], i, B, u - 1)
                    for h in range(2):
                        for t in range(KT_N):
                            at = (2 * t + h) * XA_DH
                            mm = pe.transpose(turn_ps[:, h, t * KT:(t + 1) * KT], k_hat[0:KT, at:at + XA_DH], ident[0:KT, 0:KT])
                    mm.then_inc(sem["kT_ready"], 1)
                u = s - 3
                if 0 <= u < N:
                    hold(pe, sem["wo_lo_done"], i, 1, u // B + 1)
                    hold(pe, sem["oT_lo_done"], i, B, u + 1)
                    read_out(s, i)
                    for h in range(2):
                        mm = three_products(pe, y_ps[0:T, :], oT_hi[:, u % 2, h, :], oT_lo[:, u % 2, h, :], wo_hi[:, h, :],
                                            wo_lo[:, h, :], h == 0, h == 1)
                    mm.then_inc(sem["y_ready"], 1)
                u = s
                if u < N:
                    hold(pe, sem["wv_lo_done"], i, 1, u // B + 1)
                    project(v01_ps[0:KT, 0:PW], u, 0, wv_hi, wv_lo)
                    project(v01_ps[0:KT, PW:2 * PW], u, 1, wv_hi, wv_lo).then_inc(sem["v_ready"], 1)
                u = s - 1
                if 0 <= u < N:
                    hold(pe, sem["kT_lo_done"], i, B, u + 1)
                    hold(pe, sem["q_lo_done"], i, 4, 4 * (u // B) + 2 * (u % B // HALF) + 2)
                    hold(pe, sem["exp_done"], i, 2 * B, 2 * u)
                    cols = slice(u % B * T, (u % B + 1) * T)
                    for h in range(2):
                        mm = three_products(pe, scores_ps[0:T, h, 0:KVP], qT_hi[:, h, cols], qT_lo[:, h, cols],
                                            kT_hi[:, h, :], kT_lo[:, h, :], True, True)
                    mm.then_inc(sem["scores_ready"], 1)
                u = s - 2
                if 0 <= u < N:
                    hold(pe, sem["probs_done"], i, B, u + 1)
                    if s - 1 < N:
                        hold(pe, sem["kT_lo_done"], i, B, u + 2)
                    else:
                        hold(pe, sem["oT_lo_done"], i, B, u)
                    for h in range(2):
                        for t in range(KT_N):
                            mm = pe.transpose(turn_ps[0:KT, h, t * T:(t + 1) * T], probs[0:T, u % 2, h, t * KT:(t + 1) * KT],
                                              ident[0:T, 0:T])
                    mm.then_inc(sem["probsT_ready"], 1)
                u = s
                if u < N:
                    hold(pe, sem["khat_done"], i, 2 * B, 2 * u + 2)
                    project(kv2_ps[0:KT, PW:2 * PW], u, 2, wv_hi, wv_lo).then_inc(sem["v_ready"], 1)
                u = s - 2
                if 0 <= u < N:
                    hold(pe, sem["v_copied"], i, 2 * B, 2 * u + 2)
                    for h in range(2):
                        hold(pe, sem[f"probsT_{h}_done"], i, B, u + 1)
                        for t in range(KT_N):
                            at = (2 * t + h) * XA_DH
                            mm = pe.matmul(turn_ps[:, h, 0:T], V[0:KT, u % 4, at:at + XA_DH],
                                           probsT[0:KT, u % 2, h, t * T:(t + 1) * T], start=(t == 0), stop=(t == KT_N - 1))
                    mm.then_inc(sem["o_ready"], 1)
                p, k = proj_after(s), squares_after(s)
                if p is not None:
                    hold(pe, sem["y_added"], i, B, s - 2)
                    queries(i, p)
                if k is not None:
                    hold(pe, sem["y_added"], i, B, s - 2)
                    sum_squares(i, k)
                if s == 0:
                    for b in range(B):
                        turn(pe, b)
                    pe.wait_ge(sem["turn_lo"], B)
                    queries(0, 0)
                    queries(0, 1)
                    sum_squares(0, 0)

            def read_out(s, i):
                hold(pe, sem["y_added"], i, B, s - 3)
                p, k = proj_after(s - 1), squares_after(s - 1)
                if p is not None:
                    hold(pe, sem["q_lo_done"], i, 4, p + 1)
                if k is not None:
                    hold(pe, sem["qms_done"], i, 2, k + 1)

            pe.wait_ge(sem["pads_set"], 3)
            run_slots(pe, slot, HEAD, LAG, PAIRS)


def experts(nc, env, gateT, gate_bias, w_up, w_down, out):
    resid, xT_hi, xT_lo = env["resid"], env["xT_hi"], env["xT_lo"]
    E = EXPERTS
    with ExitStack() as es:
        def sb(name, shape, dt=F32):
            return es.enter_context(nc.sbuf_tensor("ex_" + name, shape, dt))

        def ps(name, shape):
            return es.enter_context(nc.psum_tensor("ex_" + name, shape, F32))

        up_raw, down_raw = sb("up_raw", [P, DC, 2 * HID]), sb("down_raw", [P, HC, D])
        up_hi, up_lo = sb("up_hi", [P, DC, 2 * HID], F32R), sb("up_lo", [P, DC, 2 * HID], F32R)
        down_hi, down_lo = sb("down_hi", [P, HC, D], F32R), sb("down_lo", [P, HC, D], F32R)
        gate_w, gate_b = sb("gate_w", [P, DC, E]), sb("gate_b", [P, E])
        silu_g, h_full = sb("silu_g", [P, 2, HT]), sb("h_full", [P, 2, HT])
        h_hi, h_lo = sb("h_hi", [P, HC, TOK], F32R), sb("h_lo", [P, HC, TOK], F32R)
        share = sb("share", [P, B, UNITS_E])
        share_e = sb("share_e", [P, B])
        score, chosen, onehot, iota_e = (sb("score", [P, B, E]), sb("chosen", [P, B, E]), sb("onehot", [P, 2, B, E]),
                                         sb("iota_e", [P, B, E]))
        top_v, top_i, top_f = sb("top_v", [P, B, 8]), sb("top_i", [P, B, 8], U32), sb("top_f", [P, B, 8])
        total = sb("total", [P, 2, B])

        gu_ps = ps("gu_ps", [P, 2, 2, BANK])
        y_ps = ps("y_ps", [P, 2, BANK])
        turn_ps = ps("turn_ps", [P, BANK])
        logit_ps = ps("logit_ps", [P, BANK])

        names = """gate_loaded up_loaded down_loaded iota_set logits_ready logits_exp router up_hi_done up_lo_done down_hi_done
            down_lo_done up_ready silu_done mul_done h_hi_done h_lo_done y_ready share_set y_added out_ln out_mean out_pow
            out_done stored""".split()
        sem = {n: es.enter_context(nc.semaphore("ex_" + n)) for n in names + LN_SEMS + TURN_SEMS}
        ln_stats, ln_power, ln_apply = layer_norm_stages(nc, env, sem)
        last_sem = {"ln_stat": sem["out_ln"], "ln_mean": sem["out_mean"], "ln_pow": sem["out_pow"], "ln_done": sem["out_done"]}
        out_stats, out_power, out_apply = layer_norm_stages(nc, env, last_sem)
        turn, turn_high, turn_low = turn_stages(nc, env, sem, turn_ps)
        block = es.enter_context(nc.Block())

        @block.sync
        def _(sp):
            sp.dma_start(gate_w[:], gateT).then_inc(sem["gate_loaded"], 16)
            sp.dma_start(gate_b[:], gate_bias.partition_broadcast(P)).then_inc(sem["gate_loaded"], 16)
            with sp.Fori(0, UNITS_E) as e:
                sp.wait_ge(sem["up_lo_done"], e)
                sp.dma_start(up_raw[:], w_up[e]).then_inc(sem["up_loaded"], 16)
                sp.wait_ge(sem["down_lo_done"], e)
                sp.dma_start(down_raw[:, 0:2, :],
                             w_down[e, 0:2 * P, :].rearrange("(k p) n -> p k n", p=P)).then_inc(sem["down_loaded"], 16)
                sp.dma_start(down_raw[0:HID - 2 * P, 2, :], w_down[e, 2 * P:HID, :]).then_inc(sem["down_loaded"], 16)
            for b in range(B):
                sp.wait_ge(sem["out_done"], b + 1)
                sp.dma_start(out[b], resid[0:T, b, :]).then_inc(sem["stored"], 16)
            sp.wait_ge(sem["stored"], 16 * B)

        @block.gpsimd
        def _(pool):
            pool.iota(iota_e[:], [[0, B], [1, E]], base=0, channel_multiplier=0,
                      allow_small_or_imprecise_dtypes=True).then_inc(sem["iota_set"], 1)
            ln_power(pool)
            with pool.Fori(0, UNITS_E) as e:
                pool.wait_ge(sem["up_hi_done"], e + 1)
                pool.tensor_tensor(up_lo[:], up_raw[:], up_hi[:].bitcast(F32), ALU.subtract).then_inc(sem["up_lo_done"], 1)
                pool.wait_ge(sem["down_loaded"], e * 32 + 32)
                pool.wait_ge(sem["y_ready"], e * B)
                round_high(pool, down_hi[:, 0:2, :], down_raw[:, 0:2, :], env["zero"]).then_inc(sem["down_hi_done"], 1)
                round_high(pool, down_hi[0:HID - 2 * P, 2, :], down_raw[0:HID - 2 * P, 2, :], env["zero"]).then_inc(sem["down_hi_done"], 1)
                for j in range(UPS):
                    g, c = divmod(j, HC)
                    m = HID_TILES[c][1]
                    cols = slice(g * HT, (g + 1) * HT)
                    pool.wait_ge(sem["mul_done"], e * UPS + j + 1)
                    round_high(pool, h_hi[0:m, c, cols], h_full[0:m, j % 2, :], env["zero"]).then_inc(sem["h_hi_done"], 1)
                    pool.wait_ge(sem["h_hi_done"], e * UPS + j + 1)
                    pool.tensor_tensor(h_lo[0:m, c, cols], h_full[0:m, j % 2, :], h_hi[0:m, c, cols].bitcast(F32),
                                       ALU.subtract).then_inc(sem["h_lo_done"], 1)
                pool.wait_ge(sem["y_ready"], e * B + HALF)
            out_power(pool)

        @block.scalar
        def _(act):
            for b in range(B):
                turn_high(act, b)
            act.wait_ge(sem["logits_ready"], 1)
            act.activation(score[0:T].rearrange("p b e -> p (b e)"), logit_ps[0:T, 0:B * E], ACT.Exp,
                           scale=-1.0).then_inc(sem["logits_exp"], 1)
            with act.Fori(0, UNITS_E) as e:
                act.wait_ge(sem["up_loaded"], e * 16 + 16)
                act.wait_ge(sem["up_ready"], e * UPS)
                act.copy(up_hi[:], up_raw[:]).then_inc(sem["up_hi_done"], 1)
                for j in range(UPS):
                    m = HID_TILES[j % HC][1]
                    act.wait_ge(sem["up_ready"], e * UPS + j + 1)
                    if j < 2:
                        act.wait_ge(sem["mul_done"], e * UPS)
                    else:
                        act.wait_ge(sem["mul_done"], e * UPS + j - 1)
                    act.activation(silu_g[0:m, j % 2, :], gu_ps[0:m, j % 2, 0, 0:HT], ACT.Silu).then_inc(sem["silu_done"], 1)

        @block.vector
        def _(dve):
            ln_stats(dve)
            ln_apply(dve)
            for b in range(B):
                turn_low(dve, b)
            count = [0]

            def step(ins):
                count[0] += 1
                ins.then_inc(sem["router"], 1)
                dve.wait_ge(sem["router"], count[0])

            dve.wait_ge(sem["logits_exp"], 1)
            step(dve.tensor_scalar(score[0:T], score[0:T], 1.0, None, ALU.add))
            step(dve.reciprocal(score[0:T], score[0:T]))
            dve.wait_ge(sem["gate_loaded"], 32)
            step(dve.tensor_tensor(chosen[0:T], score[0:T], gate_b[0:T, :].unsqueeze(1).broadcast_to([T, B, E]), ALU.add))
            for b in range(B):
                step(dve.max(top_v[0:T, b, :], chosen[0:T, b, :]))
                step(dve.max_index(top_i[0:T, b, :], top_v[0:T, b, :], chosen[0:T, b, :]))
            step(dve.tensor_copy(top_f[0:T], top_i[0:T]))
            dve.wait_ge(sem["iota_set"], 1)
            for k in range(2):
                step(dve.tensor_tensor(onehot[0:T, k], iota_e[0:T], top_f[0:T, :, k:k + 1].broadcast_to([T, B, E]),
                                       ALU.is_equal))
            step(dve.tensor_tensor(onehot[0:T, 0], onehot[0:T, 0], onehot[0:T, 1], ALU.add))
            step(dve.tensor_tensor(onehot[0:T, 0], onehot[0:T, 0], score[0:T], ALU.mult))
            step(dve.tensor_reduce(total[0:T, 0, :], onehot[0:T, 0], AX_X, ALU.add))
            step(dve.reciprocal(total[0:T, 1, :], total[0:T, 0, :]))
            step(dve.memset(share[0:T, :, E:UNITS_E], 1.0))
            step(dve.tensor_tensor(share[0:T, :, 0:E], onehot[0:T, 0],
                                   total[0:T, 1, :].unsqueeze(2).broadcast_to([T, B, E]), ALU.mult))
            with dve.Fori(0, UNITS_E) as e:
                dve.wait_ge(sem["down_hi_done"], e * 2 + 2)
                dve.tensor_tensor(down_lo[:, 0:2, :], down_raw[:, 0:2, :], down_hi[:, 0:2, :].bitcast(F32), ALU.subtract)
                dve.tensor_tensor(down_lo[0:HID - 2 * P, 2, :], down_raw[0:HID - 2 * P, 2, :],
                                  down_hi[0:HID - 2 * P, 2, :].bitcast(F32), ALU.subtract).then_inc(sem["down_lo_done"], 1)
                dve.wait_ge(sem["y_added"], e * B)
                dve.tensor_copy(share_e[0:T, :], share[0:T, :, bass.ds(e, 1)].rearrange("p b o -> p (b o)")).then_inc(sem["share_set"], 1)
                for j in range(UPS):
                    m = HID_TILES[j % HC][1]
                    dve.wait_ge(sem["silu_done"], e * UPS + j + 1)
                    if j < 2:
                        dve.wait_ge(sem["h_lo_done"], e * UPS)
                    else:
                        dve.wait_ge(sem["h_lo_done"], e * UPS + j - 1)
                    dve.tensor_tensor(h_full[0:m, j % 2, :], silu_g[0:m, j % 2, :], gu_ps[0:m, j % 2, 1, 0:HT],
                                      ALU.mult).then_inc(sem["mul_done"], 1)
                dve.wait_ge(sem["share_set"], e + 1)
                for b in range(B):
                    dve.wait_ge(sem["y_ready"], e * B + b + 1)
                    dve.wait_ge(sem["y_added"], e * B + b)
                    dve.scalar_tensor_tensor(out=resid[0:T, b, :], in0=y_ps[0:T, b % 2, :], scalar=share_e[0:T, b:b + 1],
                                             in1=resid[0:T, b, :], op0=ALU.mult, op1=ALU.add).then_inc(sem["y_added"], 1)
            dve.wait_ge(sem["y_added"], UNITS_E * B)
            out_stats(dve)
            out_apply(dve)

        @block.tensor
        def _(pe):
            for b in range(B):
                turn(pe, b)
            pe.wait_ge(sem["turn_lo"], B)
            pe.wait_ge(sem["gate_loaded"], 32)
            for b in range(B):
                cols = slice(b * T, (b + 1) * T)
                for c in range(DC):
                    for part in (xT_hi, xT_lo):
                        mm = pe.matmul(logit_ps[0:T, b * E:(b + 1) * E], part[:, c, cols].bitcast(F32), gate_w[:, c, :],
                                       start=(c == 0 and part is xT_hi), stop=(c == DC - 1 and part is xT_lo))
            mm.then_inc(sem["logits_ready"], 1)
            with pe.Fori(0, UNITS_E) as e:
                pe.wait_ge(sem["up_lo_done"], e + 1)
                for j in range(UPS):
                    g, c = divmod(j, HC)
                    at, m = HID_TILES[c]
                    if j < 2:
                        pe.wait_ge(sem["mul_done"], e * UPS)
                    else:
                        pe.wait_ge(sem["mul_done"], e * UPS + j - 1)
                    cols = slice(g * HT, (g + 1) * HT)
                    for half in range(2):
                        w = slice(half * HID + at, half * HID + at + m)
                        for d in range(DC):
                            mm = three_products(pe, gu_ps[0:m, j % 2, half, 0:HT], up_hi[:, d, w], up_lo[:, d, w],
                                                xT_hi[:, d, cols], xT_lo[:, d, cols], d == 0, d == DC - 1)
                    mm.then_inc(sem["up_ready"], 1)
                pe.wait_ge(sem["down_lo_done"], e + 1)
                for b in range(B):
                    if b == 0:
                        pe.wait_ge(sem["h_lo_done"], e * UPS + HC)
                    if b == HALF:
                        pe.wait_ge(sem["h_lo_done"], e * UPS + UPS)
                    if b < 2:
                        pe.wait_ge(sem["y_added"], e * B)
                    else:
                        pe.wait_ge(sem["y_added"], e * B + b - 1)
                    cols = slice(b * T, (b + 1) * T)
                    for c, (_, m) in enumerate(HID_TILES):
                        mm = three_products(pe, y_ps[0:T, b % 2, :], h_hi[0:m, c, cols], h_lo[0:m, c, cols],
                                            down_hi[0:m, c, :], down_lo[0:m, c, :], c == 0, c == HC - 1)
                    mm.then_inc(sem["y_ready"], 1)


def decoder_layer(nc, xT, x, ctxT, wvT, w_quads, w_pairs, gains, gateT, gate_bias, w_up, w_down, out):
    with ExitStack() as es:
        def sb(name, shape, dt=F32):
            return es.enter_context(nc.sbuf_tensor(name, shape, dt))

        env = {
            "resid": sb("resid", [P, B, D]),
            "xT_hi": sb("xT_hi", [P, DC, TOK], F32R),
            "xT_lo": sb("xT_lo", [P, DC, TOK], F32R),
            "ident": sb("ident", [P, P]),
            "neg_half": sb("neg_half", [P, 8]),
            "ones": sb("ones", [P, 2]),
            "zero": sb("zero", [P, 1]),
            "ln_stats": sb("ln_stats", [P, B, 6]),
            "ln_mv": sb("ln_mv", [P, B, 2]),
            "ln_rstd": sb("ln_rstd", [P, B]),
        }
        with ExitStack() as ctx_es:
            for name in ("ctx_hi", "ctx_lo"):
                env[name] = ctx_es.enter_context(nc.sbuf_tensor(name, [P, CC, B * KV], F32R))
            self_attention(nc, env, xT, x, ctxT, wvT, w_quads)
            cross_attention(nc, env, w_pairs, gains)
        experts(nc, env, gateT, gate_bias, w_up, w_down, out)


def kernel(**inputs):
    import numpy as np
    import concourse.bacc as bacc
    from concourse.bass_utils import run_bass_kernel_spmd

    a = {k: np.asarray(v) for k, v in inputs.items()}

    def chunks(w):
        return w.reshape(w.shape[0] // P, P, w.shape[1]).transpose(1, 0, 2)

    x = a["x"]
    ctx = a["ctx_1024"]
    quads = []
    for q in range(QUADS):
        rows = slice(q * P, (q + 1) * P)
        quads.append(np.stack([chunks(a["L0_attn_wq"][rows].T).reshape(P, D), chunks(a["L0_attn_wk"][rows].T).reshape(P, D),
                               a["L0_attn_wo"].T[rows]], axis=1))
    pairs = []
    for q in range(PAIRS):
        cols = slice(q * PW, (q + 1) * PW)
        pairs.append(np.concatenate([chunks(a["L0_xattn_Wq"][:, cols]).reshape(P, -1),
                                     chunks(a["L0_xattn_Wk"][:, cols]).reshape(P, -1),
                                     chunks(a["L0_xattn_Wv"][:, cols]).reshape(P, -1),
                                     chunks(a["L0_xattn_Wo"][cols]).reshape(P, -1)], axis=1))
    shared_gw, shared_dw = a["L0_ffn_shared_gw"], a["L0_ffn_shared_dw"]
    ups, downs = [], []
    for e in range(EXPERTS):
        u = a["L0_ffn_up_w"][e]
        ups.append(chunks(u.T))
        downs.append(a["L0_ffn_down_w"][e].T)
    for s in range(SHARED // HID):
        rows = slice(s * HID, (s + 1) * HID)
        gu = np.concatenate([shared_gw[SHARED:][rows], shared_gw[:SHARED][rows]], axis=0)
        ups.append(chunks(gu.T))
        downs.append(shared_dw.T[rows])
    arrays = {
        "xT": chunks(x.reshape(TOK, D).T),
        "x_rows": x.transpose(1, 0, 2),
        "ctxT": chunks(ctx.reshape(B * KV, CD).T),
        "wvT": chunks(a["L0_attn_wv"].T),
        "w_quads": np.stack(quads),
        "w_pairs": np.stack(pairs),
        "gains": np.stack([a["L0_xattn_gq"], a["L0_xattn_gk"]], axis=1),
        "gateT": chunks(a["L0_ffn_gate_w"].T),
        "gate_bias": a["L0_ffn_gate_bias"],
        "w_up": np.stack(ups),
        "w_down": np.stack(downs),
    }
    arrays = {"in_" + k: np.ascontiguousarray(v) for k, v in arrays.items()}
    nc = bacc.Bacc("TRN2", target_bir_lowering=False, num_devices=1)
    aps = [nc.dram_tensor(k, v.shape, mybir.dt.from_np(v.dtype), kind="ExternalInput").ap() for k, v in arrays.items()]
    out = nc.dram_tensor("out", (B, T, D), F32, kind="ExternalOutput").ap()
    decoder_layer(nc, *aps, out)
    r = run_bass_kernel_spmd(nc, [arrays], core_ids=[0])
    return r.results[0]["out"]
```

```python
from contextlib import ExitStack

import concourse.bass as bass
from concourse import mybir

F32 = mybir.dt.float32
F32R = mybir.dt.float32r
U32 = mybir.dt.uint32
ALU = mybir.AluOpType
ACT = mybir.ActivationFunctionType
AX_X = mybir.AxisListType.X

P = 128
BANK = 512
B, T, D = 8, 112, 512
TOK = B * T
DC = D // P
HALF = B // 2
HT = HALF * T
LN_EPS = 1e-5
RMS_EPS = 1e-5
MASKED = -1.0e30

SA_HEADS, SA_DH, WINDOW = 16, 32, 64
QUAD = P // SA_DH
QUADS = SA_HEADS // QUAD
SA_SCALE = float(SA_DH) ** -0.5

XA_HEADS, XA_DH = 16, 128
KV, CD = 375, 256
CC = CD // P
KT_N = 3
KT = KV // KT_N
KVP = KV + 1
PAIRS = XA_HEADS // 2
PW = 2 * XA_DH
XA_SCALE = float(XA_DH) ** -0.5

EXPERTS, HID, SHARED = 8, 352, 704
UNITS_E = EXPERTS + SHARED // HID
HID_TILES = [(0, P), (P, P), (2 * P, HID - 2 * P)]
HC = len(HID_TILES)
UPS = 2 * HC
TILES = TOK // P


def hold(eng, sem, i, per, n):
    if isinstance(i, int) and i * per + n <= 0:
        return
    eng.wait_ge(sem, i * per + n)


def run_slots(eng, slot, head, lag, groups):
    for s in range(head):
        slot(s, 0)
    with eng.Fori(0, groups - 1) as i:
        for s in range(head, head + B):
            slot(s, i)
    for s in range(head + B * (groups - 1), lag + B * groups):
        slot(s, 0)


def round_high(pool, hi, raw, zero):
    zeros = zero[0:raw.shape[0], 0:1]
    if len(raw.shape) == 3:
        zeros = zeros.unsqueeze(2)
    return pool.tensor_tensor(hi, raw, zeros.broadcast_to(list(raw.shape)), ALU.add)


def three_products(pe, out, st_hi, st_lo, mv_hi, mv_lo, first, last):
    pe.matmul(out, st_hi, mv_hi, start=first, stop=False)
    pe.matmul(out, st_lo, mv_hi, start=False, stop=False)
    return pe.matmul(out, st_hi, mv_lo, start=False, stop=last)


def layer_norm_stages(env, sem, x, rows, tiles, groups=1):
    st, mv, rstd, half = env["ln_stats"], env["ln_mv"], env["ln_rstd"], env["neg_half"]
    ends = [tiles * (g + 1) // groups for g in range(groups)]

    def stat(dve, t):
        dve.bn_stats(st[0:rows, t, :], x[0:rows, t, :]).then_inc(sem["ln_stat"], 1)
        dve.wait_ge(sem["ln_stat"], t + 1)
        dve.bn_aggr(mv[0:rows, t, :], st[0:rows, t, :]).then_inc(sem["ln_mean"], 1)

    def power(pool):
        start = 0
        for g, end in enumerate(ends):
            part = rstd[0:rows, start:end]
            pool.wait_ge(sem["ln_mean"], end)
            pool.tensor_scalar(part, mv[0:rows, start:end, 1], LN_EPS, None, ALU.add).then_inc(sem["ln_eps"], 1)
            pool.wait_ge(sem["ln_eps"], g + 1)
            pool.tensor_tensor(part, part, half[0:rows, start:end], ALU.pow).then_inc(sem["ln_pow"], 1)
            start = end

    def apply(dve):
        for t in range(tiles):
            dve.wait_ge(sem["ln_pow"], 1 + sum(t >= end for end in ends))
            dve.tensor_scalar(x[0:rows, t, :], x[0:rows, t, :], mv[0:rows, t, 0:1], rstd[0:rows, t:t + 1],
                              ALU.subtract, ALU.mult).then_inc(sem["ln_done"], 1)

    return stat, power, apply


def turn_stages(nc, env, sem, norm_done, banks):
    resid, hi, lo, ident = env["resid"], env["xT_hi"], env["xT_lo"], env["ident"]
    views = [bank[:, 0:DC * T].rearrange("p (c t) -> p c t", c=DC) for bank in banks]

    def turn(pe, b):
        pe.wait_ge(norm_done, b + 1)
        if b >= 2:
            pe.wait_ge(sem["turn_lo"], b - 1)
        for c in range(DC):
            mm = pe.transpose(banks[b % 2][:, c * T:(c + 1) * T], resid[0:T, b, c * P:(c + 1) * P], ident[0:T, 0:T])
        mm.then_inc(sem["turned"], 1)

    def high(act, b):
        act.wait_ge(sem["turned"], b + 1)
        act.copy(hi[:, :, b * T:(b + 1) * T], views[b % 2]).then_inc(sem["turn_hi"], 1)

    def low(dve, b):
        dve.wait_ge(sem["turn_hi"], b + 1)
        dve.tensor_tensor(lo[:, :, b * T:(b + 1) * T], views[b % 2], hi[:, :, b * T:(b + 1) * T].bitcast(F32),
                          ALU.subtract).then_inc(sem["turn_lo"], 1)

    return turn, high, low


LN_SEMS = ["ln_stat", "ln_mean", "ln_eps", "ln_pow", "ln_done"]
TURN_SEMS = ["turned", "turn_hi", "turn_lo"]


def self_attention(nc, env, xT, x, ctxT, wvT, w_quads):
    LAG, HEAD = 4, 5
    N = QUADS * B
    resid, xT_hi, xT_lo, ident = env["resid"], env["xT_hi"], env["xT_lo"], env["ident"]
    ctx_hi, ctx_lo = env["ctx_hi"], env["ctx_lo"]
    ln_stat = layer_norm_stages(env, env["self_norm"], resid, T, B)[0]
    with ExitStack() as es:
        def sb(name, shape, dt=F32):
            return es.enter_context(nc.sbuf_tensor("sa_" + name, shape, dt))

        def ps(name, shape):
            return es.enter_context(nc.psum_tensor("sa_" + name, shape, F32))

        xT_raw = sb("xT_raw", [P, DC, TOK])
        ctx_raw = sb("ctx_raw", [P, CC, B // 2 * KV])
        wv_raw = sb("wv_raw", [P, DC, D])
        wv_hi, wv_lo = sb("wv_hi", [P, DC, D], F32R), sb("wv_lo", [P, DC, D], F32R)
        w_raw = sb("w_raw", [P, 3, D])
        w_hi, w_lo = sb("w_hi", [P, 3, D], F32R), sb("w_lo", [P, 3, D], F32R)
        V = sb("V", [P, B, D])
        qT, kT = sb("qT", [P, TOK]), sb("kT", [P, TOK])
        mask = sb("mask", [P, QUAD, T])
        masked = sb("masked", [P, 2, QUAD, T])
        probs = sb("probs", [P, 4, QUAD, T])
        probsT = sb("probsT", [P, 2, QUAD * T])
        o_nat = sb("o_nat", [P, 2, P])
        oT_hi, oT_lo = sb("oT_hi", [P, 2, T], F32R), sb("oT_lo", [P, 2, T], F32R)
        row_max, neg_max = sb("row_max", [P, 4, QUAD]), sb("neg_max", [P, 4, QUAD])
        row_sum, inv_sum = sb("row_sum", [P, 4, QUAD]), sb("inv_sum", [P, 4, QUAD])

        scores_ps = ps("scores_ps", [P, QUAD, BANK])
        probsT_ps = ps("probsT_ps", [P, BANK])
        o_ps = ps("o_ps", [P, BANK])
        y_ps = ps("y_ps", [P, BANK])
        proj_ps = ps("proj_ps", [P, BANK])

        names = """x_loaded qk_loaded wo_loaded ctx_loaded xT_hi_done xT_lo_done wv_hi_done wv_lo_done
            consts_set ctx_hi_done ctx_lo_done v_ready v_copied proj_ready proj_copied qk_hi_done qk_lo_done wo_hi_done
            wo_lo_done scores_ready masked_done max_ready negmax_ready exp_done probsT_ready probsT_copied o_ready inv_ready
            o_scaled oT_ready oT_hi_done oT_lo_done y_ready y_added""".split()
        names += [f"{array}_{c}_loaded" for array in ("wv", "xT") for c in range(DC)]
        sem = {n: es.enter_context(nc.semaphore("sa_" + n)) for n in names}
        block = es.enter_context(nc.Block())

        def split_qk_hi(pool, i, q):
            hold(pool, sem["qk_loaded"], i, 16, 16 * (q + 1))
            hold(pool, sem["proj_ready"], i, 4, 4 * q)
            round_high(pool, w_hi[:, 0:2, :], w_raw[:, 0:2, :], env["zero"]).then_inc(sem["qk_hi_done"], 1)

        def split_wo_hi(pool, i, q):
            hold(pool, sem["wo_loaded"], i, 16, 16 * (q + 1))
            hold(pool, sem["y_ready"], i, B, B * q)
            round_high(pool, w_hi[:, 2, :], w_raw[:, 2, :], env["zero"]).then_inc(sem["wo_hi_done"], 1)

        def proj_in(s):
            p = {1: 2, 2: 3, 6: 4, 7: 5}.get(s % B)
            if p is None or 4 * (s // B) + p >= 4 * QUADS:
                return None
            return 4 * (s // B) + p

        @block.sync
        def _(sp):
            for c in range(DC):
                sp.dma_start(wv_raw[:, c, :], wvT[:, c, :]).then_inc(sem[f"wv_{c}_loaded"], 16)
                sp.dma_start(xT_raw[:, c, :], xT[:, c, :]).then_inc(sem[f"xT_{c}_loaded"], 16)
            sp.dma_start(w_raw[:, 0:2, :], w_quads[0, :, 0:2, :]).then_inc(sem["qk_loaded"], 16)
            sp.dma_start(w_raw[:, 2, :], w_quads[0, :, 2, :]).then_inc(sem["wo_loaded"], 16)
            sp.dma_start(resid[0:T, :, :], x).then_inc(sem["x_loaded"], 16)
            sp.dma_start(ctx_raw[:], ctxT[:, :, 0:B // 2 * KV]).then_inc(sem["ctx_loaded"], 16)
            sp.wait_ge(sem["ctx_lo_done"], 1)
            sp.dma_start(ctx_raw[:], ctxT[:, :, B // 2 * KV:B * KV]).then_inc(sem["ctx_loaded"], 16)
            with sp.Fori(1, QUADS) as q:
                sp.wait_ge(sem["qk_lo_done"], q)
                sp.dma_start(w_raw[:, 0:2, :], w_quads[q, :, 0:2, :]).then_inc(sem["qk_loaded"], 16)
                sp.wait_ge(sem["wo_lo_done"], q)
                sp.dma_start(w_raw[:, 2, :], w_quads[q, :, 2, :]).then_inc(sem["wo_loaded"], 16)

        @block.gpsimd
        def _(pool):
            pool.memset(ident[:], 0.0).then_inc(sem["consts_set"], 1)
            pool.memset(mask[:], 0.0).then_inc(sem["consts_set"], 1)
            pool.memset(env["neg_half"][:], -0.5).then_inc(sem["consts_set"], 1)
            pool.memset(env["ones"][:], 1.0).then_inc(sem["consts_set"], 1)
            pool.memset(env["zero"][:], 0.0).then_inc(sem["consts_set"], 1)
            pool.wait_ge(sem["consts_set"], 5)
            pool.affine_select(out=ident[:], in_=ident[:], compare_op=ALU.not_equal, fill=1.0, base=0,
                               pattern=[[-1, P]], channel_multiplier=1).then_inc(sem["consts_set"], 1)
            pool.affine_select(out=mask[0:T], in_=mask[0:T], compare_op=ALU.is_ge, fill=MASKED, base=WINDOW // 2,
                               pattern=[[0, QUAD], [-1, T]], channel_multiplier=1).then_inc(sem["consts_set"], 1)
            split_qk_hi(pool, 0, 0)
            split_wo_hi(pool, 0, 0)
            for half in range(2):
                cols = slice(half * (B // 2) * KV, (half + 1) * (B // 2) * KV)
                pool.wait_ge(sem["ctx_loaded"], 16 * (half + 1))
                round_high(pool, ctx_hi[:, :, cols], ctx_raw[:], env["zero"]).then_inc(sem["ctx_hi_done"], 1)
                pool.wait_ge(sem["ctx_hi_done"], half + 1)
                pool.tensor_tensor(ctx_lo[:, :, cols], ctx_raw[:], ctx_hi[:, :, cols].bitcast(F32),
                                   ALU.subtract).then_inc(sem["ctx_lo_done"], 1)

            def slot(s, i):
                if s % B == 5 and s // B + 1 < QUADS:
                    split_qk_hi(pool, i, s // B + 1)
                if s % B == 4 and s // B >= 1:
                    split_wo_hi(pool, i, s // B)

            run_slots(pool, slot, HEAD, LAG, QUADS)

        @block.scalar
        def _(act):
            for c in range(DC):
                act.wait_ge(sem[f"wv_{c}_loaded"], 16)
                act.copy(wv_hi[:, c, :], wv_raw[:, c, :]).then_inc(sem["wv_hi_done"], 1)
                act.wait_ge(sem[f"xT_{c}_loaded"], 16)
                act.copy(xT_hi[:, c, :], xT_raw[:, c, :]).then_inc(sem["xT_hi_done"], 1)
            for b in range(B):
                act.wait_ge(sem["v_ready"], b + 1)
                act.copy(V[0:T, b, :], scores_ps[0:T, b % QUAD, :]).then_inc(sem["v_copied"], 1)

            def proj_out(i, p):
                hold(act, sem["proj_ready"], i, 4, p + 1)
                dst = (qT, kT)[p % 2]
                g = p // 2 % 2
                act.copy(dst[:, g * HT:(g + 1) * HT], proj_ps[:, 0:HT]).then_inc(sem["proj_copied"], 1)

            proj_out(0, 0)
            proj_out(0, 1)

            def slot(s, i):
                u = s - 4
                if u >= 0:
                    hold(act, sem["oT_ready"], i, B, u + 1)
                    hold(act, sem["y_ready"], i, B, u - 1)
                    act.copy(oT_hi[:, u % 2, :], o_ps[:, 0:T]).then_inc(sem["oT_hi_done"], 1)
                u = s - 2
                if 0 <= u < N:
                    hold(act, sem["probsT_ready"], i, B, u + 1)
                    hold(act, sem["o_ready"], i, B, u - 1)
                    act.copy(probsT[0:T, u % 2, :], probsT_ps[0:T, 0:QUAD * T]).then_inc(sem["probsT_copied"], 1)
                p = proj_in(s)
                if p is not None:
                    proj_out(i, p)
                u = s
                if u < N:
                    hold(act, sem["negmax_ready"], i, B, u + 1)
                    hold(act, sem["probsT_ready"], i, B, u - 3)
                    for r in range(QUAD):
                        act.activation(probs[0:T, u % 4, r, :], masked[0:T, u % 2, r, :], ACT.Exp,
                                       bias=neg_max[0:T, u % 4, r:r + 1], scale=SA_SCALE,
                                       accum_out=row_sum[0:T, u % 4, r:r + 1]).then_inc(sem["exp_done"], 1)

            run_slots(act, slot, HEAD, LAG, QUADS)

        @block.vector
        def _(dve):
            for c in range(DC):
                dve.wait_ge(sem["wv_hi_done"], c + 1)
                dve.tensor_tensor(wv_lo[:, c, :], wv_raw[:, c, :], wv_hi[:, c, :].bitcast(F32),
                                  ALU.subtract).then_inc(sem["wv_lo_done"], 1)
                dve.wait_ge(sem["xT_hi_done"], c + 1)
                dve.tensor_tensor(xT_lo[:, c, :], xT_raw[:, c, :], xT_hi[:, c, :].bitcast(F32),
                                  ALU.subtract).then_inc(sem["xT_lo_done"], 1)

            def split_qk_lo(i, q):
                hold(dve, sem["qk_hi_done"], i, 1, q + 1)
                dve.tensor_tensor(w_lo[:, 0:2, :], w_raw[:, 0:2, :], w_hi[:, 0:2, :].bitcast(F32),
                                  ALU.subtract).then_inc(sem["qk_lo_done"], 1)

            def split_wo_lo(i, q):
                hold(dve, sem["wo_hi_done"], i, 1, q + 1)
                dve.tensor_tensor(w_lo[:, 2, :], w_raw[:, 2, :], w_hi[:, 2, :].bitcast(F32),
                                  ALU.subtract).then_inc(sem["wo_lo_done"], 1)

            split_qk_lo(0, 0)
            split_wo_lo(0, 0)
            dve.wait_ge(sem["consts_set"], 7)
            dve.wait_ge(sem["x_loaded"], 16)

            def slot(s, i):
                u = s - 4
                if u >= 0:
                    hold(dve, sem["oT_hi_done"], i, B, u + 1)
                    dve.tensor_tensor(oT_lo[:, u % 2, :], o_ps[:, 0:T], oT_hi[:, u % 2, :].bitcast(F32),
                                      ALU.subtract).then_inc(sem["oT_lo_done"], 1)
                if s % B == 4 and s // B >= 1:
                    split_wo_lo(i, s // B)
                u = s
                if u < N:
                    hold(dve, sem["scores_ready"], i, B, u + 1)
                    hold(dve, sem["exp_done"], i, QUAD * B, QUAD * (u - 1))
                    dve.tensor_tensor(masked[0:T, u % 2], scores_ps[0:T, :, 0:T], mask[0:T],
                                      ALU.add).then_inc(sem["masked_done"], 1)
                    hold(dve, sem["masked_done"], i, B, u + 1)
                    dve.tensor_reduce(row_max[0:T, u % 4, :], masked[0:T, u % 2], AX_X, ALU.max).then_inc(sem["max_ready"], 1)
                    hold(dve, sem["max_ready"], i, B, u + 1)
                    dve.tensor_scalar(neg_max[0:T, u % 4, :], row_max[0:T, u % 4, :], -SA_SCALE, None,
                                      ALU.mult).then_inc(sem["negmax_ready"], 1)
                if s % B == 5 and s // B + 1 < QUADS:
                    split_qk_lo(i, s // B + 1)
                u = s - 2
                if 0 <= u < N:
                    hold(dve, sem["exp_done"], i, QUAD * B, QUAD * (u + 1))
                    dve.reciprocal(inv_sum[0:T, u % 4, :], row_sum[0:T, u % 4, :]).then_inc(sem["inv_ready"], 1)
                u = s - 3
                if 0 <= u < N:
                    hold(dve, sem["o_ready"], i, B, u + 1)
                    hold(dve, sem["inv_ready"], i, B, u + 1)
                    hold(dve, sem["oT_ready"], i, B, u - 1)
                    dve.tensor_tensor(o_nat[0:T, u % 2, :].rearrange("p (h d) -> p h d", h=QUAD),
                                      o_ps[0:T, 0:P].rearrange("p (h d) -> p h d", h=QUAD),
                                      inv_sum[0:T, u % 4, :].unsqueeze(2).broadcast_to([T, QUAD, SA_DH]),
                                      ALU.mult).then_inc(sem["o_scaled"], 1)
                u = s - 4
                if u >= 0:
                    hold(dve, sem["y_ready"], i, B, u + 1)
                    hold(dve, sem["y_added"], i, B, u)
                    dve.tensor_tensor(resid[0:T, u % B, :], resid[0:T, u % B, :], y_ps[0:T, :],
                                      ALU.add).then_inc(sem["y_added"], 1)
                    if u == N - B + 1:
                        ln_stat(dve, 0)
                    if u > N - B:
                        dve.wait_ge(sem["y_added"], u + 1)
                        ln_stat(dve, u % B)

            run_slots(dve, slot, HEAD, LAG, QUADS)

        @block.tensor
        def _(pe):
            for start in range(0, B, QUAD):
                for c in range(DC):
                    pe.wait_ge(sem["wv_lo_done"], c + 1)
                    pe.wait_ge(sem["xT_lo_done"], c + 1)
                    for b in range(start, start + QUAD):
                        if start and c == 0:
                            pe.wait_ge(sem["v_copied"], b - QUAD + 1)
                        cols = slice(b * T, (b + 1) * T)
                        mm = three_products(pe, scores_ps[0:T, b % QUAD, :], xT_hi[:, c, cols], xT_lo[:, c, cols],
                                            wv_hi[:, c, :], wv_lo[:, c, :], c == 0, c == DC - 1)
                        if c == DC - 1:
                            mm.then_inc(sem["v_ready"], 1)

            def project(i, p):
                hold(pe, sem["qk_lo_done"], i, 1, p // 4 + 1)
                hold(pe, sem["proj_copied"], i, 4, p)
                g = p // 2 % 2
                for c in range(DC):
                    w = slice(c * P, (c + 1) * P)
                    mm = three_products(pe, proj_ps[:, 0:HT], w_hi[:, p % 2, w], w_lo[:, p % 2, w],
                                        xT_hi[:, c, g * HT:(g + 1) * HT], xT_lo[:, c, g * HT:(g + 1) * HT],
                                        c == 0, c == DC - 1)
                mm.then_inc(sem["proj_ready"], 1)

            project(0, 0)
            project(0, 1)
            pe.wait_ge(sem["v_copied"], B)
            pe.wait_ge(sem["consts_set"], 7)

            def slot(s, i):
                u = s - 4
                if u >= 0:
                    hold(pe, sem["o_scaled"], i, B, u + 1)
                    pe.transpose(o_ps[:, 0:T], o_nat[0:T, u % 2, :], ident[0:T, 0:T]).then_inc(sem["oT_ready"], 1)
                u = s
                if u < N:
                    hold(pe, sem["proj_copied"], i, 4, 4 * (u // B) + 2 * (u % B // HALF) + 2)
                    hold(pe, sem["masked_done"], i, B, u)
                    cols = slice(u % B * T, (u % B + 1) * T)
                    for r in range(QUAD):
                        rows = slice(r * SA_DH, (r + 1) * SA_DH)
                        mm = pe.matmul(scores_ps[0:T, r, 0:T], qT[rows, cols], kT[rows, cols], start=True, stop=True)
                    mm.then_inc(sem["scores_ready"], 1)
                u = s - 2
                if 0 <= u < N:
                    hold(pe, sem["exp_done"], i, QUAD * B, QUAD * (u + 1))
                    hold(pe, sem["probsT_copied"], i, B, u)
                    for r in range(QUAD):
                        mm = pe.transpose(probsT_ps[0:T, r * T:(r + 1) * T], probs[0:T, u % 4, r, :], ident[0:T, 0:T])
                    mm.then_inc(sem["probsT_ready"], 1)
                p = proj_in(s)
                if p is not None:
                    project(i, p)
                u = s - 3
                if 0 <= u < N:
                    hold(pe, sem["probsT_copied"], i, B, u + 1)
                    hold(pe, sem["oT_lo_done"], i, B, u)
                    for r in range(QUAD):
                        head = (i + u // B) * P + r * SA_DH
                        mm = pe.matmul(o_ps[0:T, r * SA_DH:(r + 1) * SA_DH], probsT[0:T, u % 2, r * T:(r + 1) * T],
                                       V[0:T, u % B, bass.ds(head, SA_DH)], start=True, stop=True)
                    mm.then_inc(sem["o_ready"], 1)
                u = s - 4
                if u >= 0:
                    hold(pe, sem["wo_lo_done"], i, 1, u // B + 1)
                    hold(pe, sem["oT_lo_done"], i, B, u + 1)
                    hold(pe, sem["y_added"], i, B, u)
                    three_products(pe, y_ps[0:T, :], oT_hi[:, u % 2, :], oT_lo[:, u % 2, :], w_hi[:, 2, :], w_lo[:, 2, :],
                                   True, True).then_inc(sem["y_ready"], 1)

            run_slots(pe, slot, HEAD, LAG, QUADS)


def cross_attention(nc, env, w_pairs, gains):
    LAG, HEAD = 3, 3
    N = PAIRS * B
    resid, xT_hi, xT_lo, ident = env["resid"], env["xT_hi"], env["xT_lo"], env["ident"]
    ctx_hi, ctx_lo = env["ctx_hi"], env["ctx_lo"]
    ln_power, ln_apply = layer_norm_stages(env, env["self_norm"], resid, T, B)[1:]
    next_stat = layer_norm_stages(env, env["cross_norm"], resid, T, B)[0]
    with ExitStack() as es:
        def sb(name, shape, dt=F32):
            return es.enter_context(nc.sbuf_tensor("xa_" + name, shape, dt))

        def ps(name, shape):
            return es.enter_context(nc.psum_tensor("xa_" + name, shape, F32))

        wq_raw, wk_raw, wv_raw, wo_raw = (sb("wq_raw", [P, DC, PW]), sb("wk_raw", [P, CC, PW]),
                                          sb("wv_raw", [P, CC, PW]), sb("wo_raw", [P, 2, D]))
        wq_hi, wq_lo = sb("wq_hi", [P, DC, PW], F32R), sb("wq_lo", [P, DC, PW], F32R)
        wk_hi, wk_lo = sb("wk_hi", [P, CC, PW], F32R), sb("wk_lo", [P, CC, PW], F32R)
        wv_hi, wv_lo = sb("wv_hi", [P, CC, PW], F32R), sb("wv_lo", [P, CC, PW], F32R)
        wo_hi, wo_lo = sb("wo_hi", [P, 2, D], F32R), sb("wo_lo", [P, 2, D], F32R)
        gain_in, gain = sb("gain_in", [P, 2]), sb("gain", [P, 1])
        qT_hi, qT_lo = sb("qT_hi", [P, 2, TOK], F32R), sb("qT_lo", [P, 2, TOK], F32R)
        q_sq = sb("q_sq", [P, 2, HT])
        q_ms, q_scale = sb("q_ms", [P, 2, 2, HALF]), sb("q_scale", [P, 2, 2, HALF])
        k_sq, k_hat = sb("k_sq", [P, KT_N * PW]), sb("k_hat", [P, KT_N * PW])
        k_ss, k_ms, k_inv = sb("k_ss", [P, 2 * KT_N]), sb("k_ms", [P, 2 * KT_N]), sb("k_inv", [P, 2 * KT_N])
        sum_eps = sb("sum_eps", [P, 2 * KT_N])
        kT_hi, kT_lo = sb("kT_hi", [P, 2, KVP], F32R), sb("kT_lo", [P, 2, KVP], F32R)
        V = sb("V", [P, 4, KT_N * PW])
        probs = sb("probs", [P, 2, 2, KV])
        probsT = sb("probsT", [P, 2, 2, KT_N * T])
        oT_hi, oT_lo = sb("oT_hi", [P, 2, 2, T], F32R), sb("oT_lo", [P, 2, 2, T], F32R)
        row_max, bias = sb("row_max", [P, 2, 2]), sb("bias", [P, 2, 2])
        row_sum, inv_sum = sb("row_sum", [P, 2, 2]), sb("inv_sum", [P, 2, 2])

        k01_ps = ps("k01_ps", [P, BANK])
        kv2_ps = ps("kv2_ps", [P, BANK])
        v01_ps = ps("v01_ps", [P, BANK])
        turn_ps = ps("turn_ps", [P, 2, BANK])
        scores_ps = ps("scores_ps", [P, 2, BANK])
        y_ps = ps("y_ps", [P, BANK])

        names = """wq_loaded wk_loaded wv_loaded wo_loaded gains_loaded gain_ready pads_set
            wq_hi_done wq_lo_done wk_hi_done wk_lo_done wv_hi_done wv_lo_done wo_hi_done wo_lo_done
            q_ready q_hi_done q_sq_done q_lo_done qss_ready qms_done q_scale_done
            k_ready k_sq_done kss_done kms_done kinv_done khat_done v_ready v_copied
            kT_ready kT_hi_done kT_lo_done scores_ready max_done bias_ready exp_done inv_done probs_done
            probsT_ready probsT_0_done probsT_1_done o_ready oT_hi_done oT_lo_done y_ready y_added""".split()
        sem = {n: es.enter_context(nc.semaphore("xa_" + n)) for n in names + TURN_SEMS}
        turn, turn_high, turn_low = turn_stages(nc, env, sem, env["self_norm"]["ln_done"], [scores_ps[:, 0], scores_ps[:, 1]])
        block = es.enter_context(nc.Block())

        def split_hi(pool, i, q, name, raw, hi, done, per, count):
            hold(pool, sem[name + "_loaded"], i, 16, 16 * (q + 1))
            hold(pool, sem[done], i, per, count)
            round_high(pool, hi[:], raw[:], env["zero"]).then_inc(sem[name + "_hi_done"], 1)

        def split_lo(dve, i, q, name, raw, hi, lo):
            hold(dve, sem[name + "_hi_done"], i, 1, q + 1)
            dve.tensor_tensor(lo[:], raw[:], hi[:].bitcast(F32), ALU.subtract).then_inc(sem[name + "_lo_done"], 1)

        def proj_after(s):
            p = {1: 2, 2: 3, 5: 4, 6: 5}.get(s % B)
            if p is None or 4 * (s // B) + p >= 4 * PAIRS:
                return None
            return 4 * (s // B) + p

        def squares_after(s):
            k = {3: 1, 7: 2}.get(s % B)
            if k is None or 2 * (s // B) + k >= 2 * PAIRS:
                return None
            return 2 * (s // B) + k

        @block.sync
        def _(sp):
            loads = ((wk_raw, "wk", slice(4 * PW, 6 * PW)), (wv_raw, "wv", slice(6 * PW, 8 * PW)),
                     (wq_raw, "wq", slice(0, 4 * PW)), (wo_raw, "wo", slice(8 * PW, 12 * PW)))
            for raw, name, cols in loads:
                sp.dma_start(raw[:].rearrange("p a n -> p (a n)"), w_pairs[0, :, cols]).then_inc(sem[name + "_loaded"], 16)
                if name == "wq":
                    sp.dma_start(gain_in[:], gains).then_inc(sem["gains_loaded"], 16)
            with sp.Fori(1, PAIRS) as q:
                for raw, name, cols in loads[2:3] + loads[0:2] + loads[3:4]:
                    sp.wait_ge(sem[name + "_lo_done"], q)
                    sp.dma_start(raw[:].rearrange("p a n -> p (a n)"),
                                 w_pairs[q, :, cols]).then_inc(sem[name + "_loaded"], 16)

        @block.gpsimd
        def _(pool):
            pool.memset(kT_hi[:, :, KV:KVP].bitcast(F32), 0.0).then_inc(sem["pads_set"], 1)
            pool.memset(kT_lo[:, :, KV:KVP].bitcast(F32), 0.0).then_inc(sem["pads_set"], 1)
            pool.memset(sum_eps[:], XA_DH * RMS_EPS).then_inc(sem["pads_set"], 1)
            ln_power(pool)
            split_hi(pool, 0, 0, "wk", wk_raw, wk_hi, "k_ready", B, 0)
            split_hi(pool, 0, 0, "wv", wv_raw, wv_hi, "v_ready", 2 * B, 0)
            split_hi(pool, 0, 0, "wq", wq_raw, wq_hi, "q_ready", 4, 0)
            pool.wait_ge(sem["gains_loaded"], 16)
            pool.tensor_scalar(gain[:], gain_in[:, 0:1], gain_in[:, 1:2], XA_SCALE * XA_DH, ALU.mult,
                               ALU.mult).then_inc(sem["gain_ready"], 1)

            def query_scale(i, k):
                g = k % 2
                hold(pool, sem["qms_done"], i, 2, k + 1)
                hold(pool, sem["exp_done"], i, 2 * B, B * (k - 1))
                pool.tensor_tensor(q_scale[0:T, g], q_ms[0:T, g], env["neg_half"][0:T, 0:2 * HALF].rearrange(
                    "p (a b) -> p a b", a=2), ALU.pow).then_inc(sem["q_scale_done"], 1)

            def slot(s, i):
                if s % B == 0 and 1 <= s // B < PAIRS:
                    split_hi(pool, i, s // B, "wv", wv_raw, wv_hi, "v_ready", 2 * B, 2 * B * (s // B))
                u = s
                if u < N:
                    hold(pool, sem["kss_done"], i, B, u + 1)
                    pool.tensor_tensor(k_ms[0:KT, :], k_ss[0:KT, :], sum_eps[0:KT, :], ALU.add).then_inc(sem["kms_done"], 1)
                    hold(pool, sem["kms_done"], i, B, u + 1)
                    hold(pool, sem["khat_done"], i, 2 * B, 2 * u)
                    pool.tensor_tensor(k_inv[0:KT, :], k_ms[0:KT, :], env["neg_half"][0:KT, 0:2 * KT_N],
                                       ALU.pow).then_inc(sem["kinv_done"], 1)
                if s % B == 3 and s // B + 1 < PAIRS:
                    q = s // B + 1
                    split_hi(pool, i, q, "wq", wq_raw, wq_hi, "q_ready", 4, 4 * q)
                if s % B == 7 and s // B + 1 < PAIRS:
                    q = s // B + 1
                    split_hi(pool, i, q, "wk", wk_raw, wk_hi, "k_ready", 2 * B, 2 * B * q)
                u = s - 1
                if 0 <= u < N:
                    hold(pool, sem["inv_done"], i, B, u + 1)
                    pool.tensor_tensor(probs[0:T, u % 2], probs[0:T, u % 2],
                                       inv_sum[0:T, u % 2, :].unsqueeze(2).broadcast_to([T, 2, KV]),
                                       ALU.mult).then_inc(sem["probs_done"], 1)
                if s % B == 2 and s // B < PAIRS:
                    split_hi(pool, i, s // B, "wo", wo_raw, wo_hi, "y_ready", B, B * (s // B))
                k = squares_after(s)
                if k is not None:
                    query_scale(i, k)
                if s == 0:
                    query_scale(0, 0)

            run_slots(pool, slot, HEAD, LAG, PAIRS)

        @block.scalar
        def _(act):
            def queries_out(i, p):
                g, h = p // 2 % 2, p % 2
                hold(act, sem["q_ready"], i, 4, p + 1)
                act.activation(qT_hi[:, h, g * HT:(g + 1) * HT], y_ps[:, 0:HT], ACT.Copy,
                               scale=gain[:, 0:1]).then_inc(sem["q_hi_done"], 1)
                if h == 0:
                    hold(act, sem["qss_ready"], i, 2, p // 2)
                act.activation(q_sq[:, h, :], y_ps[:, 0:HT], ACT.Square).then_inc(sem["q_sq_done"], 1)

            def slot(s, i):
                u = s
                if u < N:
                    hold(act, sem["k_ready"], i, 2 * B, 2 * u + 1)
                    hold(act, sem["kss_done"], i, B, u)
                    act.activation(k_sq[0:KT, 0:2 * PW], k01_ps[0:KT, :], ACT.Square).then_inc(sem["k_sq_done"], 1)
                    hold(act, sem["k_ready"], i, 2 * B, 2 * u + 2)
                    act.activation(k_sq[0:KT, 2 * PW:3 * PW], kv2_ps[0:KT, 0:PW], ACT.Square).then_inc(sem["k_sq_done"], 1)
                u = s - 1
                if 0 <= u < N:
                    hold(act, sem["kT_ready"], i, B, u + 1)
                    act.copy(kT_hi[:, :, 0:KV], turn_ps[:, :, 0:KV]).then_inc(sem["kT_hi_done"], 1)
                u = s
                if u < N:
                    hold(act, sem["v_ready"], i, 2 * B, 2 * u + 1)
                    hold(act, sem["o_ready"], i, B, u - 3)
                    act.copy(V[0:KT, u % 4, 0:2 * PW], v01_ps[0:KT, :]).then_inc(sem["v_copied"], 1)
                u = s - 2
                if 0 <= u < N:
                    hold(act, sem["probsT_ready"], i, B, u + 1)
                    hold(act, sem["o_ready"], i, B, u - 1)
                    act.copy(probsT[0:KT, u % 2, 0, :], turn_ps[0:KT, 0, 0:KT_N * T]).then_inc(sem["probsT_0_done"], 1)
                u = s - 1
                if 0 <= u < N:
                    hold(act, sem["bias_ready"], i, B, u + 1)
                    hold(act, sem["probsT_ready"], i, B, u - 1)
                    for h in range(2):
                        act.activation(probs[0:T, u % 2, h, :], scores_ps[0:T, h, 0:KV], ACT.Exp,
                                       bias=bias[0:T, u % 2, h:h + 1],
                                       scale=q_scale[0:T, u % B // HALF, h, u % HALF:u % HALF + 1],
                                       accum_out=row_sum[0:T, u % 2, h:h + 1]).then_inc(sem["exp_done"], 1)
                u = s
                if u < N:
                    hold(act, sem["v_ready"], i, 2 * B, 2 * u + 2)
                    act.copy(V[0:KT, u % 4, 2 * PW:3 * PW], kv2_ps[0:KT, PW:2 * PW]).then_inc(sem["v_copied"], 1)
                u = s - 2
                if 0 <= u < N:
                    hold(act, sem["o_ready"], i, B, u + 1)
                    hold(act, sem["y_ready"], i, B, u - 1)
                    act.copy(oT_hi[:, u % 2], turn_ps[:, :, 0:T]).then_inc(sem["oT_hi_done"], 1)
                p = proj_after(s)
                if p is not None:
                    queries_out(i, p)
                if s == 0:
                    for b in range(B):
                        turn_high(act, b)
                    act.wait_ge(sem["gain_ready"], 1)
                    queries_out(0, 0)
                    queries_out(0, 1)

            run_slots(act, slot, HEAD, LAG, PAIRS)

        @block.vector
        def _(dve):
            ln_apply(dve)
            split_lo(dve, 0, 0, "wk", wk_raw, wk_hi, wk_lo)
            split_lo(dve, 0, 0, "wv", wv_raw, wv_hi, wv_lo)

            def queries_out(i, p):
                g, h = p // 2 % 2, p % 2
                cols = slice(g * HT, (g + 1) * HT)
                hold(dve, sem["q_sq_done"], i, 4, p + 1)
                dve.scalar_tensor_tensor(out=qT_lo[:, h, cols], in0=y_ps[:, 0:HT], scalar=gain[:, 0:1],
                                         in1=qT_hi[:, h, cols].bitcast(F32), op0=ALU.mult,
                                         op1=ALU.subtract).then_inc(sem["q_lo_done"], 1)

            def mean_squares(i, k):
                hold(dve, sem["qss_ready"], i, 2, k + 1)
                hold(dve, sem["q_scale_done"], i, 2, k - 1)
                dve.tensor_scalar(q_ms[0:T, k % 2].rearrange("p a b -> p (a b)"), y_ps[0:T, 0:2 * HALF], XA_DH * RMS_EPS,
                                  None, ALU.add).then_inc(sem["qms_done"], 1)

            def slot(s, i):
                if s % B == 0 and 1 <= s // B < PAIRS:
                    split_lo(dve, i, s // B, "wv", wv_raw, wv_hi, wv_lo)
                u = s
                if u < N:
                    hold(dve, sem["k_sq_done"], i, 2 * B, 2 * u + 2)
                    hold(dve, sem["kms_done"], i, B, u)
                    dve.tensor_reduce(k_ss[0:KT, :], k_sq[0:KT, :].rearrange("p (a d) -> p a d", d=XA_DH), AX_X,
                                      ALU.add).then_inc(sem["kss_done"], 1)
                u = s - 1
                if 0 <= u < N:
                    hold(dve, sem["kT_hi_done"], i, B, u + 1)
                    dve.tensor_tensor(kT_lo[:, :, 0:KV], turn_ps[:, :, 0:KV], kT_hi[:, :, 0:KV].bitcast(F32),
                                      ALU.subtract).then_inc(sem["kT_lo_done"], 1)
                u = s - 3
                if 0 <= u < N:
                    hold(dve, sem["y_ready"], i, B, u + 1)
                    hold(dve, sem["y_added"], i, B, u)
                    dve.tensor_tensor(resid[0:T, u % B, :], resid[0:T, u % B, :], y_ps[0:T, :],
                                      ALU.add).then_inc(sem["y_added"], 1)
                    if u >= N - B:
                        dve.wait_ge(sem["y_added"], u + 1)
                        next_stat(dve, u % B)
                u = s
                if u < N:
                    hold(dve, sem["kinv_done"], i, B, u + 1)
                    hold(dve, sem["kT_ready"], i, B, u)
                    dve.tensor_tensor(k_hat[0:KT, 0:2 * PW].rearrange("p (a d) -> p a d", d=XA_DH),
                                      k01_ps[0:KT, :].rearrange("p (a d) -> p a d", d=XA_DH),
                                      k_inv[0:KT, 0:4].unsqueeze(2).broadcast_to([KT, 4, XA_DH]),
                                      ALU.mult).then_inc(sem["khat_done"], 1)
                    dve.tensor_tensor(k_hat[0:KT, 2 * PW:3 * PW].rearrange("p (a d) -> p a d", d=XA_DH),
                                      kv2_ps[0:KT, 0:PW].rearrange("p (a d) -> p a d", d=XA_DH),
                                      k_inv[0:KT, 4:6].unsqueeze(2).broadcast_to([KT, 2, XA_DH]),
                                      ALU.mult).then_inc(sem["khat_done"], 1)
                u = s - 1
                if 0 <= u < N:
                    hold(dve, sem["scores_ready"], i, B, u + 1)
                    hold(dve, sem["bias_ready"], i, B, u)
                    dve.tensor_reduce(row_max[0:T, u % 2, :], scores_ps[0:T, :, 0:KV], AX_X, ALU.max).then_inc(sem["max_done"], 1)
                    hold(dve, sem["max_done"], i, B, u + 1)
                    hold(dve, sem["q_scale_done"], i, 2, 2 * (u // B) + u % B // HALF + 1)
                    hold(dve, sem["exp_done"], i, 2 * B, 2 * (u - 1))
                    dve.scalar_tensor_tensor(out=bias[0:T, u % 2, :], in0=row_max[0:T, u % 2, :], scalar=-1.0,
                                             in1=q_scale[0:T, u % B // HALF, :, u % HALF], op0=ALU.mult,
                                             op1=ALU.mult).then_inc(sem["bias_ready"], 1)
                u = s - 2
                if 0 <= u < N:
                    hold(dve, sem["probsT_ready"], i, B, u + 1)
                    hold(dve, sem["o_ready"], i, B, u - 1)
                    dve.tensor_copy(probsT[0:KT, u % 2, 1, :], turn_ps[0:KT, 1, 0:KT_N * T]).then_inc(sem["probsT_1_done"], 1)
                if s % B == 3 and s // B + 1 < PAIRS:
                    split_lo(dve, i, s // B + 1, "wq", wq_raw, wq_hi, wq_lo)
                if s % B == 7 and s // B + 1 < PAIRS:
                    split_lo(dve, i, s // B + 1, "wk", wk_raw, wk_hi, wk_lo)
                u = s - 1
                if 0 <= u < N:
                    hold(dve, sem["exp_done"], i, 2 * B, 2 * (u + 1))
                    hold(dve, sem["probs_done"], i, B, u - 1)
                    dve.reciprocal(inv_sum[0:T, u % 2, :], row_sum[0:T, u % 2, :]).then_inc(sem["inv_done"], 1)
                u = s - 2
                if 0 <= u < N:
                    hold(dve, sem["oT_hi_done"], i, B, u + 1)
                    dve.tensor_tensor(oT_lo[:, u % 2], turn_ps[:, :, 0:T], oT_hi[:, u % 2].bitcast(F32),
                                      ALU.subtract).then_inc(sem["oT_lo_done"], 1)
                if s % B == 2 and s // B < PAIRS:
                    split_lo(dve, i, s // B, "wo", wo_raw, wo_hi, wo_lo)
                p = proj_after(s)
                if p is not None:
                    queries_out(i, p)
                k = squares_after(s)
                if k is not None:
                    mean_squares(i, k)
                if s == 0:
                    for b in range(B):
                        turn_low(dve, b)
                    split_lo(dve, 0, 0, "wq", wq_raw, wq_hi, wq_lo)
                    dve.wait_ge(sem["gain_ready"], 1)
                    queries_out(0, 0)
                    queries_out(0, 1)
                    mean_squares(0, 0)

            run_slots(dve, slot, HEAD, LAG, PAIRS)

        @block.tensor
        def _(pe):
            def project(out, u, tile, w_hi, w_lo):
                cols = slice(u % B * KV + tile * KT, u % B * KV + (tile + 1) * KT)
                for c in range(CC):
                    mm = three_products(pe, out, ctx_hi[:, c, cols], ctx_lo[:, c, cols], w_hi[:, c, :], w_lo[:, c, :],
                                        c == 0, c == CC - 1)
                return mm

            def queries(i, p):
                g, h = p // 2 % 2, p % 2
                hold(pe, sem["wq_lo_done"], i, 1, p // 4 + 1)
                hold(pe, sem["q_lo_done"], i, 4, p)
                for c in range(DC):
                    w = slice(h * XA_DH, (h + 1) * XA_DH)
                    mm = three_products(pe, y_ps[:, 0:HT], wq_hi[:, c, w], wq_lo[:, c, w],
                                        xT_hi[:, c, g * HT:(g + 1) * HT], xT_lo[:, c, g * HT:(g + 1) * HT],
                                        c == 0, c == DC - 1)
                mm.then_inc(sem["q_ready"], 1)

            def sum_squares(i, k):
                hold(pe, sem["q_sq_done"], i, 4, 2 * k + 2)
                hold(pe, sem["q_lo_done"], i, 4, 2 * k + 2)
                for h in range(2):
                    for b in range(HALF):
                        at = h * HALF + b
                        mm = pe.matmul(y_ps[0:T, at:at + 1], q_sq[:, h, b * T:(b + 1) * T], env["ones"][:, 0:1],
                                       start=True, stop=True)
                mm.then_inc(sem["qss_ready"], 1)

            def slot(s, i):
                u = s
                if u < N:
                    hold(pe, sem["wk_lo_done"], i, 1, u // B + 1)
                    hold(pe, sem["khat_done"], i, 2 * B, 2 * u)
                    project(k01_ps[0:KT, 0:PW], u, 0, wk_hi, wk_lo)
                    project(k01_ps[0:KT, PW:2 * PW], u, 1, wk_hi, wk_lo).then_inc(sem["k_ready"], 1)
                    hold(pe, sem["v_copied"], i, 2 * B, 2 * u)
                    project(kv2_ps[0:KT, 0:PW], u, 2, wk_hi, wk_lo).then_inc(sem["k_ready"], 1)
                u = s - 1
                if 0 <= u < N:
                    hold(pe, sem["khat_done"], i, 2 * B, 2 * u + 2)
                    hold(pe, sem["oT_lo_done"], i, B, u - 1)
                    for h in range(2):
                        for t in range(KT_N):
                            at = (2 * t + h) * XA_DH
                            mm = pe.transpose(turn_ps[:, h, t * KT:(t + 1) * KT], k_hat[0:KT, at:at + XA_DH], ident[0:KT, 0:KT])
                    mm.then_inc(sem["kT_ready"], 1)
                u = s - 3
                if 0 <= u < N:
                    hold(pe, sem["wo_lo_done"], i, 1, u // B + 1)
                    hold(pe, sem["oT_lo_done"], i, B, u + 1)
                    read_out(s, i)
                    for h in range(2):
                        mm = three_products(pe, y_ps[0:T, :], oT_hi[:, u % 2, h, :], oT_lo[:, u % 2, h, :], wo_hi[:, h, :],
                                            wo_lo[:, h, :], h == 0, h == 1)
                    mm.then_inc(sem["y_ready"], 1)
                u = s
                if u < N:
                    hold(pe, sem["wv_lo_done"], i, 1, u // B + 1)
                    project(v01_ps[0:KT, 0:PW], u, 0, wv_hi, wv_lo)
                    project(v01_ps[0:KT, PW:2 * PW], u, 1, wv_hi, wv_lo).then_inc(sem["v_ready"], 1)
                u = s - 1
                if 0 <= u < N:
                    hold(pe, sem["kT_lo_done"], i, B, u + 1)
                    hold(pe, sem["q_lo_done"], i, 4, 4 * (u // B) + 2 * (u % B // HALF) + 2)
                    hold(pe, sem["exp_done"], i, 2 * B, 2 * u)
                    cols = slice(u % B * T, (u % B + 1) * T)
                    for h in range(2):
                        mm = three_products(pe, scores_ps[0:T, h, 0:KVP], qT_hi[:, h, cols], qT_lo[:, h, cols],
                                            kT_hi[:, h, :], kT_lo[:, h, :], True, True)
                    mm.then_inc(sem["scores_ready"], 1)
                u = s - 2
                if 0 <= u < N:
                    hold(pe, sem["probs_done"], i, B, u + 1)
                    if s - 1 < N:
                        hold(pe, sem["kT_lo_done"], i, B, u + 2)
                    else:
                        hold(pe, sem["oT_lo_done"], i, B, u)
                    for h in range(2):
                        for t in range(KT_N):
                            mm = pe.transpose(turn_ps[0:KT, h, t * T:(t + 1) * T], probs[0:T, u % 2, h, t * KT:(t + 1) * KT],
                                              ident[0:T, 0:T])
                    mm.then_inc(sem["probsT_ready"], 1)
                u = s
                if u < N:
                    hold(pe, sem["khat_done"], i, 2 * B, 2 * u + 2)
                    project(kv2_ps[0:KT, PW:2 * PW], u, 2, wv_hi, wv_lo).then_inc(sem["v_ready"], 1)
                u = s - 2
                if 0 <= u < N:
                    hold(pe, sem["v_copied"], i, 2 * B, 2 * u + 2)
                    for h in range(2):
                        hold(pe, sem[f"probsT_{h}_done"], i, B, u + 1)
                        for t in range(KT_N):
                            at = (2 * t + h) * XA_DH
                            mm = pe.matmul(turn_ps[:, h, 0:T], V[0:KT, u % 4, at:at + XA_DH],
                                           probsT[0:KT, u % 2, h, t * T:(t + 1) * T], start=(t == 0), stop=(t == KT_N - 1))
                    mm.then_inc(sem["o_ready"], 1)
                p, k = proj_after(s), squares_after(s)
                if p is not None:
                    hold(pe, sem["y_added"], i, B, s - 2)
                    queries(i, p)
                if k is not None:
                    hold(pe, sem["y_added"], i, B, s - 2)
                    sum_squares(i, k)
                if s == 0:
                    for b in range(B):
                        turn(pe, b)
                    pe.wait_ge(sem["turn_lo"], B)
                    queries(0, 0)
                    queries(0, 1)
                    sum_squares(0, 0)

            def read_out(s, i):
                hold(pe, sem["y_added"], i, B, s - 3)
                p, k = proj_after(s - 1), squares_after(s - 1)
                if p is not None:
                    hold(pe, sem["q_lo_done"], i, 4, p + 1)
                if k is not None:
                    hold(pe, sem["qms_done"], i, 2, k + 1)

            pe.wait_ge(sem["pads_set"], 3)
            run_slots(pe, slot, HEAD, LAG, PAIRS)


def experts(nc, env, gateT, gate_bias, w_up, w_down, out):
    resid, xT_hi, xT_lo, ident = env["resid"], env["xT_hi"], env["xT_lo"], env["ident"]
    E, LAST = EXPERTS, UNITS_E - 1
    with ExitStack() as es:
        def sb(name, shape, dt=F32):
            return es.enter_context(nc.sbuf_tensor("ex_" + name, shape, dt))

        def ps(name, shape):
            return es.enter_context(nc.psum_tensor("ex_" + name, shape, F32))

        rows = sb("rows", [P, TILES, D])
        up_raw, down_raw = sb("up_raw", [P, DC, 2 * HID]), sb("down_raw", [P, HC, D])
        up_hi, up_lo = sb("up_hi", [P, DC, 2 * HID], F32R), sb("up_lo", [P, DC, 2 * HID], F32R)
        down_hi, down_lo = sb("down_hi", [P, HC, D], F32R), sb("down_lo", [P, HC, D], F32R)
        gate_w, gate_b = sb("gate_w", [P, DC, E]), sb("gate_b", [P, E])
        gate_hi, gate_lo = sb("gate_hi", [P, DC, E], F32R), sb("gate_lo", [P, DC, E], F32R)
        logitsT = sb("logitsT", [E, TOK])
        silu_g, h_full = sb("silu_g", [P, 2, HT]), sb("h_full", [P, 2, HT])
        h_hi, h_lo = sb("h_hi", [P, HC, TOK], F32R), sb("h_lo", [P, HC, TOK], F32R)
        share = sb("share", [P, TILES, UNITS_E])
        share_e = sb("share_e", [P, TILES])
        score, chosen, onehot, iota_e = (sb("score", [P, TILES, E]), sb("chosen", [P, TILES, E]),
                                         sb("onehot", [P, 2, TILES, E]), sb("iota_e", [P, TILES, E]))
        top_v, top_i, top_f = sb("top_v", [P, TILES, 8]), sb("top_i", [P, TILES, 8], U32), sb("top_f", [P, TILES, 8])
        total = sb("total", [P, 2, TILES])

        gu_ps = ps("gu_ps", [P, 2, 2, BANK])
        y_ps = ps("y_ps", [P, 2, BANK])
        turn_ps = ps("turn_ps", [P, 2, BANK])

        names = """gate_loaded up_loaded down_loaded rows_moved iota_set gate_hi_done gate_lo_done logitsT_ready
            logitsT_copied logits_ready logits_exp router up_hi_done up_lo_done down_hi_done down_lo_done up_ready silu_done
            mul_done h_hi_done h_lo_done y_ready share_set y_added stored""".split()
        sem = {n: es.enter_context(nc.semaphore("ex_" + n)) for n in names + LN_SEMS + TURN_SEMS}
        ln_power, ln_apply = layer_norm_stages(env, env["cross_norm"], resid, T, B)[1:]
        out_stat, out_power, out_apply = layer_norm_stages(env, sem, rows, P, TILES, groups=2)
        turn, turn_high, turn_low = turn_stages(nc, env, sem, env["cross_norm"]["ln_done"], [turn_ps[:, 0], turn_ps[:, 1]])
        cuts = sorted({b * T for b in range(B + 1)} | {t * P for t in range(TILES + 1)})
        pieces = list(zip(cuts[:-1], cuts[1:]))

        def over_experts(eng, expert):
            expert(0)
            with eng.Fori(1, LAST) as e:
                expert(e)
            expert(LAST)

        def is_at(e, n):
            return isinstance(e, int) and e == n

        block = es.enter_context(nc.Block())

        @block.sync
        def _(sp):
            def load(e):
                hold(sp, sem["up_lo_done"], e, 1, 0)
                sp.dma_start(up_raw[:], w_up[e]).then_inc(sem["up_loaded"], 16)
                if is_at(e, 0):
                    sp.dma_start(gate_w[:], gateT).then_inc(sem["gate_loaded"], 16)
                    sp.dma_start(gate_b[:], gate_bias.partition_broadcast(P)).then_inc(sem["gate_loaded"], 16)
                hold(sp, sem["down_lo_done"], e, 1, 0)
                sp.dma_start(down_raw[:, 0:2, :],
                             w_down[e, 0:2 * P, :].rearrange("(k p) n -> p k n", p=P)).then_inc(sem["down_loaded"], 16)
                sp.dma_start(down_raw[0:HID - 2 * P, 2, :], w_down[e, 2 * P:HID, :]).then_inc(sem["down_loaded"], 16)
                if is_at(e, 0):
                    for a, z in pieces:
                        sp.wait_ge(env["cross_norm"]["ln_done"], a // T + 1)
                        sp.dma_start(rows[a % P:a % P + z - a, a // P, :],
                                     resid[a % T:a % T + z - a, a // T, :]).then_inc(sem["rows_moved"], 16)

            over_experts(sp, load)
            flat = out.rearrange("b t d -> (b t) d")
            for t in range(TILES):
                sp.wait_ge(sem["ln_done"], t + 1)
                sp.dma_start(flat[t * P:(t + 1) * P, :], rows[:, t, :]).then_inc(sem["stored"], 16)
            sp.wait_ge(sem["stored"], 16 * TILES)

        @block.gpsimd
        def _(pool):
            ln_power(pool)
            pool.iota(iota_e[:], [[0, TILES], [1, E]], base=0, channel_multiplier=0,
                      allow_small_or_imprecise_dtypes=True).then_inc(sem["iota_set"], 1)

            def expert(e):
                pool.wait_ge(sem["up_hi_done"], e + 1)
                pool.tensor_tensor(up_lo[:], up_raw[:], up_hi[:].bitcast(F32), ALU.subtract).then_inc(sem["up_lo_done"], 1)
                if is_at(e, 0):
                    pool.wait_ge(sem["gate_loaded"], 32)
                    round_high(pool, gate_hi[:], gate_w[:], env["zero"]).then_inc(sem["gate_hi_done"], 1)
                    pool.wait_ge(sem["gate_hi_done"], 1)
                    pool.tensor_tensor(gate_lo[:], gate_w[:], gate_hi[:].bitcast(F32),
                                       ALU.subtract).then_inc(sem["gate_lo_done"], 1)
                pool.wait_ge(sem["down_loaded"], e * 32 + 32)
                hold(pool, sem["y_ready"], e, TILES, 0)
                round_high(pool, down_hi[:, 0:2, :], down_raw[:, 0:2, :], env["zero"]).then_inc(sem["down_hi_done"], 1)
                round_high(pool, down_hi[0:HID - 2 * P, 2, :], down_raw[0:HID - 2 * P, 2, :],
                           env["zero"]).then_inc(sem["down_hi_done"], 1)
                for j in range(UPS):
                    g, c = divmod(j, HC)
                    m = HID_TILES[c][1]
                    cols = slice(g * HT, (g + 1) * HT)
                    pool.wait_ge(sem["mul_done"], e * UPS + j + 1)
                    round_high(pool, h_hi[0:m, c, cols], h_full[0:m, j % 2, :], env["zero"]).then_inc(sem["h_hi_done"], 1)
                    pool.wait_ge(sem["h_hi_done"], e * UPS + j + 1)
                    pool.tensor_tensor(h_lo[0:m, c, cols], h_full[0:m, j % 2, :], h_hi[0:m, c, cols].bitcast(F32),
                                       ALU.subtract).then_inc(sem["h_lo_done"], 1)

            over_experts(pool, expert)
            out_power(pool)

        @block.scalar
        def _(act):
            def expert(e):
                act.wait_ge(sem["up_loaded"], e * 16 + 16)
                hold(act, sem["up_ready"], e, UPS, 0)
                act.copy(up_hi[:], up_raw[:]).then_inc(sem["up_hi_done"], 1)
                if is_at(e, 0):
                    for b in range(B):
                        turn_high(act, b)
                for j in range(UPS):
                    m = HID_TILES[j % HC][1]
                    act.wait_ge(sem["up_ready"], e * UPS + j + 1)
                    hold(act, sem["mul_done"], e, UPS, max(j - 1, 0))
                    act.activation(silu_g[0:m, j % 2, :], gu_ps[0:m, j % 2, 0, 0:HT], ACT.Silu).then_inc(sem["silu_done"], 1)
                    if is_at(e, 0) and j == HC - 1:
                        for g in range(2):
                            act.wait_ge(sem["logitsT_ready"], g + 1)
                            act.copy(logitsT[:, g * HT:(g + 1) * HT], turn_ps[0:E, g, 0:HT]).then_inc(sem["logitsT_copied"], 1)
                if is_at(e, 0):
                    act.wait_ge(sem["logits_ready"], 1)
                    act.activation(score[:].rearrange("p b e -> p (b e)"), turn_ps[:, 0, 0:TILES * E], ACT.Exp,
                                   scale=-1.0).then_inc(sem["logits_exp"], 1)

            over_experts(act, expert)

        @block.vector
        def _(dve):
            ln_apply(dve)
            for b in range(B):
                turn_low(dve, b)

            def router():
                count = [0]

                def step(ins):
                    count[0] += 1
                    ins.then_inc(sem["router"], 1)
                    dve.wait_ge(sem["router"], count[0])

                dve.wait_ge(sem["logits_exp"], 1)
                step(dve.tensor_scalar(score[:], score[:], 1.0, None, ALU.add))
                step(dve.reciprocal(score[:], score[:]))
                dve.wait_ge(sem["gate_loaded"], 32)
                step(dve.tensor_tensor(chosen[:], score[:], gate_b[:].unsqueeze(1).broadcast_to([P, TILES, E]), ALU.add))
                for t in range(TILES):
                    dve.max(top_v[:, t, :], chosen[:, t, :]).then_inc(sem["router"], 1)
                count[0] += TILES
                dve.wait_ge(sem["router"], count[0])
                for t in range(TILES):
                    dve.max_index(top_i[:, t, :], top_v[:, t, :], chosen[:, t, :]).then_inc(sem["router"], 1)
                count[0] += TILES
                dve.wait_ge(sem["router"], count[0])
                step(dve.tensor_copy(top_f[:], top_i[:]))
                dve.wait_ge(sem["iota_set"], 1)
                for k in range(2):
                    step(dve.tensor_tensor(onehot[:, k], iota_e[:], top_f[:, :, k:k + 1].broadcast_to([P, TILES, E]),
                                           ALU.is_equal))
                step(dve.tensor_tensor(onehot[:, 0], onehot[:, 0], onehot[:, 1], ALU.add))
                step(dve.tensor_tensor(onehot[:, 0], onehot[:, 0], score[:], ALU.mult))
                step(dve.tensor_reduce(total[:, 0, :], onehot[:, 0], AX_X, ALU.add))
                step(dve.reciprocal(total[:, 1, :], total[:, 0, :]))
                step(dve.memset(share[:, :, E:UNITS_E], 1.0))
                step(dve.tensor_tensor(share[:, :, 0:E], onehot[:, 0],
                                       total[:, 1, :].unsqueeze(2).broadcast_to([P, TILES, E]), ALU.mult))

            def expert(e):
                dve.wait_ge(sem["down_hi_done"], e * 2 + 2)
                dve.tensor_tensor(down_lo[:, 0:2, :], down_raw[:, 0:2, :], down_hi[:, 0:2, :].bitcast(F32), ALU.subtract)
                dve.tensor_tensor(down_lo[0:HID - 2 * P, 2, :], down_raw[0:HID - 2 * P, 2, :],
                                  down_hi[0:HID - 2 * P, 2, :].bitcast(F32), ALU.subtract).then_inc(sem["down_lo_done"], 1)
                for j in range(UPS):
                    m = HID_TILES[j % HC][1]
                    dve.wait_ge(sem["silu_done"], e * UPS + j + 1)
                    hold(dve, sem["h_lo_done"], e, UPS, max(j - 1, 0))
                    dve.tensor_tensor(h_full[0:m, j % 2, :], silu_g[0:m, j % 2, :], gu_ps[0:m, j % 2, 1, 0:HT],
                                      ALU.mult).then_inc(sem["mul_done"], 1)
                if is_at(e, 0):
                    router()
                hold(dve, sem["y_added"], e, TILES, 0)
                dve.tensor_copy(share_e[:], share[:, :, bass.ds(e, 1)].rearrange("p b o -> p (b o)")).then_inc(sem["share_set"], 1)
                dve.wait_ge(sem["share_set"], e + 1)
                if is_at(e, 0):
                    dve.wait_ge(sem["rows_moved"], 16 * len(pieces))
                for t in range(TILES):
                    dve.wait_ge(sem["y_ready"], e * TILES + t + 1)
                    hold(dve, sem["y_added"], e, TILES, t)
                    dve.scalar_tensor_tensor(out=rows[:, t, :], in0=y_ps[:, t % 2, :], scalar=share_e[:, t:t + 1],
                                             in1=rows[:, t, :], op0=ALU.mult, op1=ALU.add).then_inc(sem["y_added"], 1)
                    if is_at(e, LAST):
                        dve.wait_ge(sem["y_added"], e * TILES + t + 1)
                        out_stat(dve, t)

            over_experts(dve, expert)
            out_apply(dve)

        @block.tensor
        def _(pe):
            for b in range(B):
                turn(pe, b)
            pe.wait_ge(sem["turn_lo"], B)

            def logits_T():
                pe.wait_ge(sem["gate_lo_done"], 1)
                for g in range(2):
                    cols = slice(g * HT, (g + 1) * HT)
                    for c in range(DC):
                        mm = three_products(pe, turn_ps[0:E, g, 0:HT], gate_hi[:, c, :], gate_lo[:, c, :],
                                            xT_hi[:, c, cols], xT_lo[:, c, cols], c == 0, c == DC - 1)
                    mm.then_inc(sem["logitsT_ready"], 1)

            def logits():
                pe.wait_ge(sem["logitsT_copied"], 2)
                for t in range(TILES):
                    mm = pe.transpose(turn_ps[:, 0, t * E:(t + 1) * E], logitsT[:, t * P:(t + 1) * P], ident[0:E, 0:E])
                mm.then_inc(sem["logits_ready"], 1)

            def expert(e):
                pe.wait_ge(sem["up_lo_done"], e + 1)
                for j in range(UPS):
                    g, c = divmod(j, HC)
                    at, m = HID_TILES[c]
                    hold(pe, sem["mul_done"], e, UPS, max(j - 1, 0))
                    cols = slice(g * HT, (g + 1) * HT)
                    for half in range(2):
                        w = slice(half * HID + at, half * HID + at + m)
                        for d in range(DC):
                            mm = three_products(pe, gu_ps[0:m, j % 2, half, 0:HT], up_hi[:, d, w], up_lo[:, d, w],
                                                xT_hi[:, d, cols], xT_lo[:, d, cols], d == 0, d == DC - 1)
                    mm.then_inc(sem["up_ready"], 1)
                    if is_at(e, 0) and j == HC - 1:
                        logits_T()
                    if is_at(e, 0) and j == UPS - 2:
                        logits()
                pe.wait_ge(sem["down_lo_done"], e + 1)
                for t in range(TILES):
                    if t == 0:
                        pe.wait_ge(sem["h_lo_done"], e * UPS + HC)
                    if t == HT // P:
                        pe.wait_ge(sem["h_lo_done"], e * UPS + UPS)
                    hold(pe, sem["y_added"], e, TILES, max(t - 1, 0))
                    cols = slice(t * P, (t + 1) * P)
                    for c, (_, m) in enumerate(HID_TILES):
                        mm = three_products(pe, y_ps[:, t % 2, :], h_hi[0:m, c, cols], h_lo[0:m, c, cols],
                                            down_hi[0:m, c, :], down_lo[0:m, c, :], c == 0, c == HC - 1)
                    mm.then_inc(sem["y_ready"], 1)

            over_experts(pe, expert)


def decoder_layer(nc, xT, x, ctxT, wvT, w_quads, w_pairs, gains, gateT, gate_bias, w_up, w_down, out):
    with ExitStack() as es:
        def sb(name, shape, dt=F32):
            return es.enter_context(nc.sbuf_tensor(name, shape, dt))

        env = {
            "resid": sb("resid", [P, B, D]),
            "xT_hi": sb("xT_hi", [P, DC, TOK], F32R),
            "xT_lo": sb("xT_lo", [P, DC, TOK], F32R),
            "ident": sb("ident", [P, P]),
            "neg_half": sb("neg_half", [P, 8]),
            "ones": sb("ones", [P, 2]),
            "zero": sb("zero", [P, 1]),
            "ln_stats": sb("ln_stats", [P, B, 6]),
            "ln_mv": sb("ln_mv", [P, B, 2]),
            "ln_rstd": sb("ln_rstd", [P, B]),
        }
        for norm in ("self_norm", "cross_norm"):
            env[norm] = {n: es.enter_context(nc.semaphore(f"{norm}_{n}")) for n in LN_SEMS}
        with ExitStack() as ctx_es:
            for name in ("ctx_hi", "ctx_lo"):
                env[name] = ctx_es.enter_context(nc.sbuf_tensor(name, [P, CC, B * KV], F32R))
            self_attention(nc, env, xT, x, ctxT, wvT, w_quads)
            cross_attention(nc, env, w_pairs, gains)
        experts(nc, env, gateT, gate_bias, w_up, w_down, out)


def kernel(**inputs):
    import numpy as np
    import concourse.bacc as bacc
    from concourse.bass_utils import run_bass_kernel_spmd

    a = {k: np.asarray(v) for k, v in inputs.items()}

    def chunks(w):
        return w.reshape(w.shape[0] // P, P, w.shape[1]).transpose(1, 0, 2)

    x = a["x"]
    ctx = a["ctx_1024"]
    quads = []
    for q in range(QUADS):
        rows = slice(q * P, (q + 1) * P)
        quads.append(np.stack([chunks(a["L0_attn_wq"][rows].T).reshape(P, D), chunks(a["L0_attn_wk"][rows].T).reshape(P, D),
                               a["L0_attn_wo"].T[rows]], axis=1))
    pairs = []
    for q in range(PAIRS):
        cols = slice(q * PW, (q + 1) * PW)
        pairs.append(np.concatenate([chunks(a["L0_xattn_Wq"][:, cols]).reshape(P, -1),
                                     chunks(a["L0_xattn_Wk"][:, cols]).reshape(P, -1),
                                     chunks(a["L0_xattn_Wv"][:, cols]).reshape(P, -1),
                                     chunks(a["L0_xattn_Wo"][cols]).reshape(P, -1)], axis=1))
    shared_gw, shared_dw = a["L0_ffn_shared_gw"], a["L0_ffn_shared_dw"]
    ups, downs = [], []
    for e in range(EXPERTS):
        u = a["L0_ffn_up_w"][e]
        ups.append(chunks(u.T))
        downs.append(a["L0_ffn_down_w"][e].T)
    for s in range(SHARED // HID):
        rows = slice(s * HID, (s + 1) * HID)
        gu = np.concatenate([shared_gw[SHARED:][rows], shared_gw[:SHARED][rows]], axis=0)
        ups.append(chunks(gu.T))
        downs.append(shared_dw.T[rows])
    arrays = {
        "xT": chunks(x.reshape(TOK, D).T),
        "x_rows": x.transpose(1, 0, 2),
        "ctxT": chunks(ctx.reshape(B * KV, CD).T),
        "wvT": chunks(a["L0_attn_wv"].T),
        "w_quads": np.stack(quads),
        "w_pairs": np.stack(pairs),
        "gains": np.stack([a["L0_xattn_gq"], a["L0_xattn_gk"]], axis=1),
        "gateT": chunks(a["L0_ffn_gate_w"].T),
        "gate_bias": a["L0_ffn_gate_bias"],
        "w_up": np.stack(ups),
        "w_down": np.stack(downs),
    }
    arrays = {"in_" + k: np.ascontiguousarray(v) for k, v in arrays.items()}
    nc = bacc.Bacc("TRN2", target_bir_lowering=False, num_devices=1)
    aps = [nc.dram_tensor(k, v.shape, mybir.dt.from_np(v.dtype), kind="ExternalInput").ap() for k, v in arrays.items()]
    out = nc.dram_tensor("out", (B, T, D), F32, kind="ExternalOutput").ap()
    decoder_layer(nc, *aps, out)
    r = run_bass_kernel_spmd(nc, [arrays], core_ids=[0])
    return r.results[0]["out"]
```
